# Optimizing a Trainium2 kernel written in Bass

```python
import numpy as np
import jax
import jax.numpy as jnp

def _softmax(x, axis=-1):
    return jax.nn.softmax(x, axis=axis)

def _gelu(x):
    return jax.nn.gelu(x, approximate=True)

def _silu(x):
    return jax.nn.silu(x)

def _sigmoid(x):
    return jax.nn.sigmoid(x)

def _layernorm(x, axis=-1, eps=1e-05):
    m = jnp.mean(x, axis=axis, keepdims=True)
    v = jnp.var(x, axis=axis, keepdims=True)
    return (x - m) / jnp.sqrt(v + eps)

def _scatter_add(tgt, idx, src, axis=0):
    return tgt.at[idx].add(src)

def _segment_sum(src, seg, n):
    return jax.ops.segment_sum(src, seg, n)
kernel_name = 'mk_xattn_ffn_d2_seqx_r4_06b957'

def setup_inputs(seed: int=0):
    np.random.seed(seed)
    _w = jnp.asarray

    def _rec_inputs():
        import jax
        import jax.numpy as jnp
        _rk = jax.random.key(seed)
        x = -0.000125 + 0.9999 * jax.random.normal(jax.random.fold_in(_rk, 1), (4, 512, 512), jnp.float32)
        _lenS = 512 - jax.random.randint(jax.random.fold_in(_rk, 7), (4,), 0, max(1, 512 // 4) + 1, jnp.int32)
        _lenS2 = 512 - jax.random.randint(jax.random.fold_in(_rk, 8), (4,), 0, max(1, 512 // 4) + 1, jnp.int32)
        fside_BxS2xS2_0 = -3.05549e-07 + 0.0199987 * jax.random.normal(jax.random.fold_in(_rk, 11), (4, 512, 512), jnp.float32)
        _ctx_1024P = jax.random.normal(jax.random.fold_in(_rk, 12), (4, 16, 256), jnp.float32)
        _ctx_1024c = jax.random.dirichlet(jax.random.fold_in(_rk, 512), 0.3 * jnp.ones((16,), jnp.float32), (4, 512))
        _ctx_1024t = jnp.einsum('bsk,bkd->bsd', _ctx_1024c, _ctx_1024P)
        _ctx_1024t = _ctx_1024t * jax.lax.rsqrt(jnp.mean(jnp.square(_ctx_1024t)) + 1e-12) * 0.953939
        ctx_1024 = 6.82029e-06 + 0.0200006 * (_ctx_1024t + 0.3 * jax.random.normal(jax.random.fold_in(_rk, 612), (4, 512, 256), jnp.float32))
        return (x, fside_BxS2xS2_0, ctx_1024)
    x, fside_BxS2xS2_0, ctx_1024 = _rec_inputs()

    def _L0_xattn_setup():
        import jax, jax.numpy as jnp
        import numpy as np
        EPS = 1e-06
        QMAX = 127.0

        def _smooth_quant_linear(x, w):
            amax_x = jnp.max(jnp.abs(x), axis=0)
            amax_w = jnp.max(jnp.abs(w), axis=0)
            s = jnp.sqrt(jnp.maximum(amax_x, EPS) / jnp.maximum(amax_w, EPS))
            s = jnp.maximum(s, EPS)
            xs = x / s
            ws = w * s
            x_scale = jnp.maximum(jnp.max(jnp.abs(xs), axis=-1, keepdims=True), EPS) / QMAX
            w_scale = jnp.maximum(jnp.max(jnp.abs(ws), axis=-1, keepdims=True), EPS) / QMAX
            x_q = jnp.clip(jnp.round(xs / x_scale), -QMAX, QMAX)
            w_q = jnp.clip(jnp.round(ws / w_scale), -QMAX, QMAX)
            return x_q @ w_q.T * x_scale * w_scale.T

        def _expert_forward(xe, guw, dw):
            h = _smooth_quant_linear(xe, guw)
            gate, up = jnp.split(h, 2, axis=-1)
            a = jax.nn.silu(gate) * up
            return _smooth_quant_linear(a, dw)
        key = jax.random.key(seed)
        k1, k2, k3 = jax.random.split(key, 3)
        E, T, D, I = (8, 512, 512, 256)
        x = jax.random.normal(k1, (E, T, D), dtype=jnp.float32)
        gate_up_weight = jax.random.normal(k2, (E, 2 * I, D), dtype=jnp.float32) * 0.02
        down_weight = jax.random.normal(k3, (E, D, I), dtype=jnp.float32) * 0.02
        return {'x': x, 'gate_up_weight': gate_up_weight, 'down_weight': down_weight}
    _L0_xattn_all = _L0_xattn_setup()
    _L0_xattn_in = {k: v for k, v in _L0_xattn_all.items() if k in ()}
    del _L0_xattn_all

    def _L0_ffn_setup():
        import jax, jax.numpy as jnp
        import numpy as np
        HIDDEN = 512
        INTER = 1376
        LUT_SIZE = 16

        def _ghost_linear(x, idx, lut):
            w = lut[idx]
            return jnp.einsum('bsh,oh->bso', x, w)
        key = jax.random.key(seed)
        k_x, k_lut, k_g, k_u, k_d = jax.random.split(key, 5)
        x = jax.random.normal(k_x, (2, 1024, HIDDEN), dtype=jnp.float32)
        lut = jax.random.normal(k_lut, (LUT_SIZE,), dtype=jnp.float32) * 0.02
        gate_idx = jax.random.randint(k_g, (INTER, HIDDEN), 0, LUT_SIZE, dtype=jnp.int32)
        up_idx = jax.random.randint(k_u, (INTER, HIDDEN), 0, LUT_SIZE, dtype=jnp.int32)
        down_idx = jax.random.randint(k_d, (HIDDEN, INTER), 0, LUT_SIZE, dtype=jnp.int32)
        return {'x': x, 'lut': lut, 'gate_idx': gate_idx, 'up_idx': up_idx, 'down_idx': down_idx}
    _L0_ffn_all = _L0_ffn_setup()
    _L0_ffn_in = {k: v for k, v in _L0_ffn_all.items() if k in ('lut', 'gate_idx', 'up_idx', 'down_idx')}
    del _L0_ffn_all

    def _L1_xattn_setup():
        import jax, jax.numpy as jnp
        import numpy as np
        B_, L_, D_MODEL = (4, 512, 256)
        D_STATE, D_CONV, EXPAND = (16, 4, 2)
        D_INNER = EXPAND * D_MODEL
        DT_RANK = (D_MODEL + 15) // 16

        def silu(x):
            return x * jax.nn.sigmoid(x)
        key = jax.random.key(seed)
        ks = jax.random.split(key, 10)
        f32 = jnp.float32
        hidden_states = jax.random.normal(ks[0], (B_, L_, D_MODEL), dtype=f32)
        z = jax.random.normal(ks[1], (B_, D_INNER, L_), dtype=f32)
        in_proj_w = jax.random.normal(ks[2], (D_INNER, D_MODEL), dtype=f32) * 0.02
        conv_w = jax.random.normal(ks[3], (D_INNER, 1, D_CONV), dtype=f32) * 0.1
        conv_b = jax.random.normal(ks[4], (D_INNER,), dtype=f32) * 0.02
        x_proj_w = jax.random.normal(ks[5], (DT_RANK + 2 * D_STATE, D_INNER), dtype=f32) * 0.02
        dt_proj_w = jax.random.uniform(ks[6], (D_INNER, DT_RANK), dtype=f32, minval=-DT_RANK ** (-0.5), maxval=DT_RANK ** (-0.5))
        dt = jnp.exp(jax.random.uniform(ks[7], (D_INNER,), dtype=f32, minval=np.log(0.001), maxval=np.log(0.1)))
        dt_proj_b = jnp.log(jnp.expm1(dt))
        A_log = jnp.log(jnp.broadcast_to(jnp.arange(1, D_STATE + 1, dtype=f32), (D_INNER, D_STATE)))
        D = jnp.ones((D_INNER,), f32)
        return {'hidden_states': hidden_states, 'z': z, 'in_proj_w': in_proj_w, 'conv_w': conv_w, 'conv_b': conv_b, 'x_proj_w': x_proj_w, 'dt_proj_w': dt_proj_w, 'dt_proj_b': dt_proj_b, 'A_log': A_log, 'D': D}
    _L1_xattn_all = _L1_xattn_setup()
    _L1_xattn_in = {k: v for k, v in _L1_xattn_all.items() if k in ('in_proj_w', 'conv_w', 'conv_b', 'x_proj_w', 'dt_proj_w', 'dt_proj_b', 'A_log', 'D')}
    del _L1_xattn_all

    def _L1_ffn_setup():
        import jax, jax.numpy as jnp
        import numpy as np
        HIDDEN = 512
        INTER = 192
        N_EXPERTS = 32
        TOP_K = 8
        key = jax.random.key(seed)
        k = jax.random.split(key, 5)
        s = 1.0 / np.sqrt(HIDDEN)
        return {'hidden_states': jax.random.normal(k[0], (1, 256, HIDDEN), jnp.float32), 'gate_w': jax.random.normal(k[1], (HIDDEN, N_EXPERTS), jnp.float32) * s, 'w_gate': jax.random.normal(k[2], (N_EXPERTS, HIDDEN, INTER), jnp.float32) * s, 'w_up': jax.random.normal(k[3], (N_EXPERTS, HIDDEN, INTER), jnp.float32) * s, 'w_down': jax.random.normal(k[4], (N_EXPERTS, INTER, HIDDEN), jnp.float32) * (1.0 / np.sqrt(INTER))}
    _L1_ffn_all = _L1_ffn_setup()
    _L1_ffn_in = {k: v for k, v in _L1_ffn_all.items() if k in ('gate_w', 'w_gate', 'w_up', 'w_down')}
    del _L1_ffn_all
    return {'x': x, 'fside_BxS2xS2_0': fside_BxS2xS2_0, 'ctx_1024': ctx_1024, 'L0_ffn_lut': _L0_ffn_in['lut'], 'L0_ffn_gate_idx': _L0_ffn_in['gate_idx'], 'L0_ffn_up_idx': _L0_ffn_in['up_idx'], 'L0_ffn_down_idx': _L0_ffn_in['down_idx'], 'L1_xattn_in_proj_w': _L1_xattn_in['in_proj_w'], 'L1_xattn_conv_w': _L1_xattn_in['conv_w'], 'L1_xattn_conv_b': _L1_xattn_in['conv_b'], 'L1_xattn_x_proj_w': _L1_xattn_in['x_proj_w'], 'L1_xattn_dt_proj_w': _L1_xattn_in['dt_proj_w'], 'L1_xattn_dt_proj_b': _L1_xattn_in['dt_proj_b'], 'L1_xattn_A_log': _L1_xattn_in['A_log'], 'L1_xattn_D': _L1_xattn_in['D'], 'L1_ffn_gate_w': _L1_ffn_in['gate_w'], 'L1_ffn_w_gate': _L1_ffn_in['w_gate'], 'L1_ffn_w_up': _L1_ffn_in['w_up'], 'L1_ffn_w_down': _L1_ffn_in['w_down']}

def reference(x, fside_BxS2xS2_0, ctx_1024, L0_ffn_lut, L0_ffn_gate_idx, L0_ffn_up_idx, L0_ffn_down_idx, L1_xattn_in_proj_w, L1_xattn_conv_w, L1_xattn_conv_b, L1_xattn_x_proj_w, L1_xattn_dt_proj_w, L1_xattn_dt_proj_b, L1_xattn_A_log, L1_xattn_D, L1_ffn_gate_w, L1_ffn_w_gate, L1_ffn_w_up, L1_ffn_w_down):
    import jax
    import jax.numpy as jnp

    def _L0_xattn_ref(x, gate_up_weight, down_weight):
        import jax, jax.numpy as jnp
        import numpy as np
        EPS = 1e-06
        QMAX = 127.0

        def _smooth_quant_linear(x, w):
            amax_x = jnp.max(jnp.abs(x), axis=0)
            amax_w = jnp.max(jnp.abs(w), axis=0)
            s = jnp.sqrt(jnp.maximum(amax_x, EPS) / jnp.maximum(amax_w, EPS))
            s = jnp.maximum(s, EPS)
            xs = x / s
            ws = w * s
            x_scale = jnp.maximum(jnp.max(jnp.abs(xs), axis=-1, keepdims=True), EPS) / QMAX
            w_scale = jnp.maximum(jnp.max(jnp.abs(ws), axis=-1, keepdims=True), EPS) / QMAX
            x_q = jnp.clip(jnp.round(xs / x_scale), -QMAX, QMAX)
            w_q = jnp.clip(jnp.round(ws / w_scale), -QMAX, QMAX)
            return x_q @ w_q.T * x_scale * w_scale.T

        def _expert_forward(xe, guw, dw):
            h = _smooth_quant_linear(xe, guw)
            gate, up = jnp.split(h, 2, axis=-1)
            a = jax.nn.silu(gate) * up
            return _smooth_quant_linear(a, dw)
        return jax.vmap(_expert_forward)(x, gate_up_weight, down_weight)

    def _L0_ffn_ref(x, lut, gate_idx, up_idx, down_idx):
        import jax, jax.numpy as jnp
        import numpy as np
        HIDDEN = 512
        INTER = 1376
        LUT_SIZE = 16

        def _ghost_linear(x, idx, lut):
            w = lut[idx]
            return jnp.einsum('bsh,oh->bso', x, w)
        gate = _ghost_linear(x, gate_idx, lut)
        up = _ghost_linear(x, up_idx, lut)
        h = jax.nn.silu(gate) * up
        return _ghost_linear(h, down_idx, lut)

    def _L1_xattn_ref(hidden_states, z, in_proj_w, conv_w, conv_b, x_proj_w, dt_proj_w, dt_proj_b, A_log, D):
        import jax, jax.numpy as jnp
        import numpy as np
        B_, L_, D_MODEL = (4, 512, 256)
        D_STATE, D_CONV, EXPAND = (16, 4, 2)
        D_INNER = EXPAND * D_MODEL
        DT_RANK = (D_MODEL + 15) // 16

        def silu(x):
            return x * jax.nn.sigmoid(x)
        Bsz, L, _ = hidden_states.shape
        d_inner, _, d_conv = conv_w.shape
        dt_rank = dt_proj_w.shape[1]
        d_state = A_log.shape[1]
        x = jnp.einsum('bld,ed->bel', hidden_states, in_proj_w)
        xc = jax.lax.conv_general_dilated(x, conv_w, window_strides=(1,), padding=[(d_conv - 1, 0)], feature_group_count=d_inner, dimension_numbers=('NCH', 'OIH', 'NCH'))
        x = silu(xc + conv_b[None, :, None])
        x_dbl = jnp.einsum('bdl,ed->bel', x, x_proj_w)
        dt_low, Bm, Cm = jnp.split(x_dbl, [dt_rank, dt_rank + d_state], axis=1)
        dt = jnp.einsum('brl,dr->bdl', dt_low, dt_proj_w)
        dt = jax.nn.softplus(dt + dt_proj_b[None, :, None])
        A = -jnp.exp(A_log)
        dt_t = jnp.moveaxis(dt, -1, 0)
        B_t = jnp.moveaxis(Bm, -1, 0)
        C_t = jnp.moveaxis(Cm, -1, 0)
        u_t = jnp.moveaxis(x, -1, 0)

        def step(state, inp):
            d, b, c, u = inp
            dA = jnp.exp(d[..., None] * A)
            state = state * dA + (d * u)[..., None] * b[:, None, :]
            y = jnp.einsum('bdn,bn->bd', state, c)
            return (state, y)
        state0 = jnp.zeros((Bsz, d_inner, d_state), x.dtype)
        _, ys = jax.lax.scan(step, state0, (dt_t, B_t, C_t, u_t))
        y = jnp.moveaxis(ys, 0, 2)
        y = y + D[None, :, None] * x
        y = y * silu(z)
        return jnp.swapaxes(y, 1, 2)

    def _L1_ffn_ref(hidden_states, gate_w, w_gate, w_up, w_down):
        import jax, jax.numpy as jnp
        import numpy as np
        HIDDEN = 512
        INTER = 192
        N_EXPERTS = 32
        TOP_K = 8
        B, S, H = hidden_states.shape
        E = gate_w.shape[1]
        x = hidden_states.reshape(-1, H)
        T = x.shape[0]
        K = TOP_K
        P = T * K
        C = 2 * (P // E)
        probs = jax.nn.softmax(x @ gate_w, axis=-1)
        w, sel = jax.lax.top_k(probs, K)
        w = w / jnp.sum(w, axis=-1, keepdims=True)
        flat_e = sel.reshape(-1)
        flat_t = jnp.repeat(jnp.arange(T), K)
        flat_w = w.reshape(-1)
        order = jnp.argsort(flat_e)
        se = flat_e[order]
        start = jnp.searchsorted(se, jnp.arange(E))
        pos = jnp.arange(P) - start[se]
        slot = jnp.where(pos < C, se * C + pos, E * C)
        slot_pair = jnp.full((E * C,), P, dtype=jnp.int32).at[slot].set(order.astype(jnp.int32), mode='drop')
        t_slot = jnp.concatenate([flat_t, jnp.array([T])])[slot_pair]
        w_slot = jnp.concatenate([flat_w, jnp.zeros((1,), flat_w.dtype)])[slot_pair]
        x_pad = jnp.concatenate([x, jnp.zeros((1, H), x.dtype)], axis=0)
        xg = x_pad[t_slot].reshape(E, C, H)
        g = jnp.einsum('ech,ehi->eci', xg, w_gate)
        u = jnp.einsum('ech,ehi->eci', xg, w_up)
        y = jnp.einsum('eci,eih->ech', jax.nn.silu(g) * u, w_down).reshape(E * C, H)
        out = jnp.zeros((T + 1, H), x.dtype).at[t_slot].add(w_slot[:, None] * y)
        return out[:T].reshape(B, S, H)
    x = x + _L0_xattn_ref(_layernorm(x, axis=-1), fside_BxS2xS2_0, ctx_1024)
    x = x + _L0_ffn_ref(_layernorm(x, axis=-1), L0_ffn_lut, L0_ffn_gate_idx, L0_ffn_up_idx, L0_ffn_down_idx)
    x = x + _L1_xattn_ref(ctx_1024, _layernorm(x, axis=-1), L1_xattn_in_proj_w, L1_xattn_conv_w, L1_xattn_conv_b, L1_xattn_x_proj_w, L1_xattn_dt_proj_w, L1_xattn_dt_proj_b, L1_xattn_A_log, L1_xattn_D)
    x = x + _L1_ffn_ref(_layernorm(x, axis=-1), L1_ffn_gate_w, L1_ffn_w_gate, L1_ffn_w_up, L1_ffn_w_down)
    return x

_drawn_inputs = setup_inputs


def setup_inputs(seed=0):
    import zlib

    import numpy as np

    out = dict(_drawn_inputs(seed))
    spreads = {'L1_xattn_D': (1.0, 0.6)}
    factors = {'L1_xattn_in_proj_w': 8.0,
     'L1_xattn_conv_w': 8.0,
     'L1_xattn_conv_b': 5.569,
     'L1_xattn_x_proj_w': 8.0,
     'L1_xattn_dt_proj_w': 8.0,
     'L1_xattn_dt_proj_b': 8.0,
     'L1_xattn_A_log': 8.0}
    for name, (base, spread) in spreads.items():
        noise = np.random.default_rng([zlib.crc32(name.encode()), seed]).standard_normal(out[name].shape)
        drawn = base * np.exp(spread * noise) if base else spread * noise
        out[name] = jnp.asarray(drawn.astype(out[name].dtype))
    for name, factor in factors.items():
        out[name] = (out[name] * factor).astype(out[name].dtype)
    return out
```

```python
from contextlib import ExitStack

import concourse.bass as bass
from concourse import mybir

P = 128
F32 = mybir.dt.float32
F32R = mybir.dt.float32r
BF16 = mybir.dt.bfloat16
I32 = mybir.dt.int32
U32 = mybir.dt.uint32
ALU = mybir.AluOpType
ACT = mybir.ActivationFunctionType
AX_X = mybir.AxisListType.X

NB, S, D = 4, 512, 512
DC = D // P
TT = S // P
DM = 256
MC = DM // P
NST = 16
RANK = 16
XD = RANK + 2 * NST
INTER = 1376
CH = -(-INTER // P)
LAST = INTER - (CH - 1) * P
WCH = 2 * D + D
EPS = 1e-5


class Link:

    def __init__(self, eng, sem, base=0):
        self.eng, self.sem, self.base, self.n = eng, sem, base, 0

    def __call__(self, ins):
        ins.then_inc(self.sem, 1)
        self.n += 1
        self.eng.wait_ge(self.sem, self.base + self.n)


def need(eng, sem, n):
    eng.wait_ge(sem, n + 1)


def start_at_one(nc, sems):
    with nc.Block() as block:
        @block.sync
        def _(sp):
            for x in sems:
                sp.sem_inc(x, 1)


def prepare_block(nc, d, s):
    with ExitStack() as ctx:
        sems = []

        def sb(name, shape, dt):
            return ctx.enter_context(nc.sbuf_tensor("look_" + name, shape, dt))

        def sem(name):
            sems.append(ctx.enter_context(nc.semaphore("look_" + name)))
            return sems[-1]

        idx = sb("idx", [P, WCH], I32)
        bit0 = sb("bit0", [P, WCH], I32)
        bits = [sb(f"bit{k}", [P, WCH], I32) for k in (1, 2, 3)]
        fence = sb("fence", [P, 1], F32)
        leaf = [sb(f"leaf{j}", [P, WCH], U32) for j in range(8)]
        lut = sb("lut", [P, 16], F32)
        lutx = sb("lutx", [P, 8], U32)
        whi = sb("whi", [P, WCH], F32R)
        wlo = sb("wlo", [P, WCH], F32R)

        ctxT = sb("ctxT", [P, MC, S], F32)
        inT = sb("inT", [P, MC, D], F32)
        xpT = sb("xpT", [P, DC, XD], F32)
        dpT = sb("dpT", [RANK, D], F32)
        convw = sb("convw", [P, DC, 4], F32)
        convb = sb("convb", [P, DC], F32)
        dtb = sb("dtb", [P, DC], F32)
        one = sb("one_col", [P, 1], F32)
        minus_one = sb("minus_one_col", [P, 1], F32)
        taps = sb("taps", [P, 4, S], F32)
        u = sb("u_all", [P, DC, S], F32)
        xd = sb("xd", [XD, S], F32)
        v = sb("v_all", [P, DC, S], F32)
        e = sb("e_all", [P, DC, S], F32)
        ln = sb("ln_all", [P, DC, S], F32)
        w1 = sb("w1_all", [P, DC, S], F32)
        psX = ctx.enter_context(nc.psum_tensor("look_psX", [P, DC, S], F32))
        psV = ctx.enter_context(nc.psum_tensor("look_psV", [P, DC, S], F32))

        consts_in = sem("consts_in")
        lut_in = sem("lut_in")
        idx_in = sem("idx_in")
        masks_made = sem("masks_made")
        lutx_made = sem("lutx_made")
        chosen = sem("chosen")
        split_made = sem("split_made")
        w_out = sem("w_out")
        ctx_in = ctx.enter_context(nc.semaphore("look_ctx_in"))
        proj_out = ctx.enter_context(nc.semaphore("look_proj_out"))
        stored = sem("stored")
        one_made = sem("one_made")
        x_ready = sem("x_ready")
        taps_ready = sem("taps_ready")
        conv_made = sem("conv_made")
        pool_link = sem("pool_link")
        act_link = sem("act_link")
        u_ready = sem("u_ready")
        xd_ready = sem("xd_ready")
        xd_copied = sem("xd_copied")
        dt_ready = sem("dt_ready")
        v_ready = sem("v_ready")
        one_added = sem("one_added")
        e_ready = sem("e_ready")
        ln_ready = sem("ln_ready")
        relu_ready = sem("relu_ready")
        delta_ready = sem("delta_ready")
        du_ready = sem("du_ready")
        bc_out = sem("bc_out")

        start_at_one(nc, sems)
        block = ctx.enter_context(nc.Block())

        @block.sync
        def _(sp):
            sp.dma_start(lut[:, :], d["lut"].rearrange("(a n) -> a n", a=1).to_broadcast([P, 16])).then_inc(lut_in, 16)
            sp.dma_start(idx[:, :], d["idx"][0]).then_inc(idx_in, 16)
            with sp.Fori(0, CH - 1) as i:
                need(sp, masks_made, 4 * i + 4)
                sp.dma_start(idx[:, :], d["idx"][i + 1]).then_inc(idx_in, 16)
                need(sp, split_made, 2 * i + 2)
                sp.dma_start(s["W"][i][:, 0:WCH], whi[:, :].bitcast(F32)).then_inc(w_out, 16)
                sp.dma_start(s["W"][i][:, WCH:2 * WCH], wlo[:, :].bitcast(F32)).then_inc(w_out, 16)
            need(sp, split_made, 2 * CH)
            sp.dma_start(s["W"][CH - 1][:, 0:WCH], whi[:, :].bitcast(F32)).then_inc(w_out, 16)
            sp.dma_start(s["W"][CH - 1][:, WCH:2 * WCH], wlo[:, :].bitcast(F32)).then_inc(w_out, 16)
            need(sp, w_out, 32 * CH)

        @block.vector
        def _(dve):
            need(dve, lut_in, 16)
            lb = lut[:, :].bitcast(U32).rearrange("p (j k) -> p j k", k=2)
            nc.vector.tensor_tensor(lutx[:, :], lb[:, :, 0], lb[:, :, 1], ALU.bitwise_xor).then_inc(lutx_made, 1)
            CHOICES = 8 + 4 + 2 + 1
            with dve.Fori(0, CH) as i:
                need(dve, lutx_made, 1)
                need(dve, idx_in, 16 * i + 16)
                nc.vector.tensor_scalar(bit0[:, :], idx[:, :], 31, 31, ALU.logical_shift_left,
                                        ALU.arith_shift_right).then_inc(masks_made, 1)
                for k in range(3):
                    nc.vector.tensor_scalar(bits[k][:, :], idx[:, :], 2 << k, None,
                                            ALU.bitwise_and).then_inc(masks_made, 1)
                need(dve, masks_made, 4 * i + 4)
                for j in range(8):
                    nc.vector.tensor_scalar(leaf[j][:, :], bit0[:, :].bitcast(U32), lutx[:, j:j + 1],
                                            lb[:, j, 0:1], ALU.bitwise_and, ALU.bitwise_xor).then_inc(chosen, 1)
                below = 8
                for k, step in enumerate((1, 2, 4)):
                    need(dve, chosen, CHOICES * i + below)
                    nc.vector.memset(fence[:, :], 0.0)
                    for j in range(0, 8, 2 * step):
                        nc.vector.copy_predicated(leaf[j][:, :], bits[k][:, :], leaf[j + step][:, :]).then_inc(chosen, 1)
                        below += 1
                need(dve, chosen, CHOICES * i + CHOICES)
                need(dve, w_out, 32 * i)
                nc.vector.tensor_copy(whi[:, :], leaf[0][:, :].bitcast(F32)).then_inc(split_made, 1)
                need(dve, split_made, 2 * i + 1)
                nc.vector.tensor_tensor(wlo[:, :], leaf[0][:, :].bitcast(F32), whi[:, :].bitcast(F32),
                                        ALU.subtract).then_inc(split_made, 1)
                need(dve, split_made, 2 * i + 2)

        @block.tensor
        def _(pe):
            need(pe, consts_in, 16 * 6)
            with pe.Fori(0, NB) as b:
                pe.wait_ge(ctx_in, 16 * b + 16)
                need(pe, taps_ready, 4 * b)
                for m in range(DC):
                    for k in range(MC):
                        last = nc.tensor.matmul(psX[:, m, :], inT[:, k, m * P:(m + 1) * P], ctxT[:, k, :],
                                                start=(k == 0), stop=(k == MC - 1))
                    last.then_inc(x_ready, 1)
                need(pe, u_ready, b + 1)
                for k in range(DC):
                    last = nc.tensor.matmul(psV[0:XD, 0, :], xpT[:, k, :], u[:, k, :], start=(k == 0), stop=(k == DC - 1))
                last.then_inc(xd_ready, 1)
                need(pe, xd_copied, b + 1)
                for m in range(DC):
                    nc.tensor.matmul(psV[:, m, :], dpT[:, m * P:(m + 1) * P], xd[0:RANK, :],
                                     start=True, stop=True).then_inc(dt_ready, 1)

        @block.scalar
        def _(act):
            act.dma_start(inT[:, :, :], d["inT"].rearrange("(k p) n -> p k n", p=P)).then_inc(consts_in, 16)
            act.dma_start(xpT[:, :, :], d["xpT"].rearrange("(k p) n -> p k n", p=P)).then_inc(consts_in, 16)
            act.dma_start(dpT[:, :], d["dpT"]).then_inc(consts_in, 16)
            act.dma_start(convw[:, :, :], d["convw"].rearrange("(c p) k -> p c k", p=P)).then_inc(consts_in, 16)
            act.dma_start(convb[:, :], d["convb"]).then_inc(consts_in, 16)
            act.dma_start(dtb[:, :], d["dtb"]).then_inc(consts_in, 16)
            need(act, consts_in, 16 * 6)
            need(act, one_made, 5)
            with act.Fori(0, NB) as b:
                for m in range(DC):
                    need(act, x_ready, DC * b + m + 1)
                    need(act, conv_made, DC * b + m)
                    for k in range(4):
                        late = 3 - k
                        if k == 3:
                            last = nc.scalar.activation(taps[:, k, :], psX[:, m, :], ACT.Identity,
                                                        bias=convb[:, m:m + 1], scale=convw[:, m, k:k + 1])
                        else:
                            last = nc.scalar.activation(taps[:, k, late:S], psX[:, m, 0:S - late], ACT.Copy,
                                                        scale=convw[:, m, k:k + 1])
                    last.then_inc(taps_ready, 1)
                need(act, conv_made, DC * b + DC)
                need(act, stored, b)
                nc.scalar.activation(u[:, :, :], v[:, :, :], ACT.Silu).then_inc(u_ready, 1)
                need(act, xd_ready, b + 1)
                need(act, bc_out, 16 * b)
                nc.scalar.activation(xd[:, :], psV[0:XD, 0, :], ACT.Copy).then_inc(xd_copied, 1)
                need(act, u_ready, b + 1)
                for m in range(DC):
                    need(act, dt_ready, DC * b + m + 1)
                    nc.scalar.activation(v[:, m, :], psV[:, m, :], ACT.Identity, bias=dtb[:, m:m + 1]).then_inc(v_ready, 1)
                need(act, v_ready, DC * b + DC)
                nc.scalar.activation(w1[:, :, :], v[:, :, :], ACT.Abs).then_inc(act_link, 1)
                need(act, act_link, b + 1)
                nc.scalar.activation(e[:, :, :], w1[:, :, :], ACT.Exp, scale=-1.0).then_inc(e_ready, 1)
                need(act, e_ready, b + 1)
                nc.scalar.activation(w1[:, :, :], e[:, :, :], ACT.Identity, bias=one[:, :]).then_inc(one_added, 1)
                need(act, one_added, 2 * b + 1)
                nc.scalar.activation(w1[:, :, :], w1[:, :, :], ACT.Identity, bias=minus_one[:, :]).then_inc(one_added, 1)
                nc.scalar.activation(ln[:, :, :], e[:, :, :], ACT.Ln, bias=one[:, :]).then_inc(ln_ready, 1)
                nc.scalar.activation(v[:, :, :], v[:, :, :], ACT.Relu).then_inc(relu_ready, 1)
                need(act, xd_copied, b + 1)
                act.dma_start(s["BC"][b], xd[RANK:XD, :]).then_inc(bc_out, 16)
            need(act, bc_out, 16 * NB)

        @block.gpsimd
        def _(pool):
            nc.gpsimd.memset(one[:, :], 1.0).then_inc(one_made, 1)
            nc.gpsimd.memset(minus_one[:, :], -1.0).then_inc(one_made, 1)
            for k in range(3):
                nc.gpsimd.memset(taps[:, k, 0:3 - k], 0.0).then_inc(one_made, 1)
            PER = 2 * DC + 2
            with pool.Fori(0, NB) as b:
                link = Link(pool, pool_link, b * PER + 1)
                need(pool, x_ready, DC * b)
                pool.dma_start(ctxT[:, :, :], d["ctxT"][b].rearrange("(k p) n -> p k n", p=P)).then_inc(ctx_in, 16)
                need(pool, delta_ready, b)
                for m in range(DC):
                    need(pool, taps_ready, DC * b + m + 1)
                    link(nc.gpsimd.tensor_tensor(taps[:, 3, :], taps[:, 3, :], taps[:, 2, :], ALU.add))
                    link(nc.gpsimd.tensor_tensor(taps[:, 3, :], taps[:, 3, :], taps[:, 1, :], ALU.add))
                    nc.gpsimd.tensor_tensor(v[:, m, :], taps[:, 3, :], taps[:, 0, :], ALU.add).then_inc(conv_made, 1)
                need(pool, one_added, 2 * b + 2)
                link(nc.gpsimd.tensor_tensor(w1[:, :, :], e[:, :, :], w1[:, :, :], ALU.subtract))
                need(pool, ln_ready, b + 1)
                link(nc.gpsimd.tensor_tensor(w1[:, :, :], ln[:, :, :], w1[:, :, :], ALU.add))
                need(pool, relu_ready, b + 1)
                nc.gpsimd.tensor_tensor(v[:, :, :], v[:, :, :], w1[:, :, :], ALU.add).then_inc(delta_ready, 1)
                need(pool, delta_ready, b + 1)
                nc.gpsimd.tensor_tensor(w1[:, :, :], v[:, :, :], u[:, :, :], ALU.mult).then_inc(du_ready, 1)
                need(pool, du_ready, b + 1)
                pool.dma_start(s["U"][b], u[:, :, :]).then_inc(proj_out, 16)
                pool.dma_start(s["DT"][b], v[:, :, :]).then_inc(proj_out, 16)
                pool.dma_start(s["DU"][b], w1[:, :, :]).then_inc(proj_out, 16)
                pool.wait_ge(proj_out, 48 * b + 48)
                pool.sem_inc(stored, 1)


MAGIC = 1.5 * 2.0 ** 23
QMAX = 127.0
QEPS = 1e-6
GU = 256


def quant_block(nc, d, s):
    with ExitStack() as ctx:
        def sb(name, shape, dt):
            return ctx.enter_context(nc.sbuf_tensor("quant_" + name, shape, dt))

        def sem(name):
            return ctx.enter_context(nc.semaphore("quant_" + name))

        ident = sb("ident", [P, P], F32)
        identb = sb("identb", [P, P], BF16)
        ones = sb("ones", [P, P], F32)
        eps = sb("eps_col", [P, 1], F32)
        magic = sb("magic_col", [P, 1], F32)
        xt = sb("xt", [P, TT, D], F32)
        wt = sb("wt", [P, TT, D], F32)
        ct = sb("ct", [P, TT, GU], F32)
        xn = sb("xn", [P, TT, D], F32)
        a = sb("a", [P, TT, GU], F32)
        sg = sb("sg", [P, TT, GU], F32)
        h = sb("h", [P, TT, D], F32)
        xs = sb("xs", [P, TT, D], F32)
        ws = sb("ws", [P, TT, D], F32)
        xq = sb("xq", [P, TT, D], BF16)
        wq = sb("wq", [P, TT, D], BF16)
        xqT = sb("xqT", [P, DC, S], BF16)
        wqT = sb("wqT", [P, DC, S], BF16)
        dg = sb("dg", [P, 3, DC, P], F32)
        wscB = sb("wscB", [P, S], F32)
        xo = sb("xo", [P, TT, D], F32)
        stats = sb("stats", [P, TT, 6], F32)
        mv = sb("mv", [P, TT, 2], F32)
        rstd = sb("rstd", [P, TT], F32)
        nmr = sb("nmr", [P, TT], F32)
        ax = sb("ax", [P, DC], F32)
        aw = sb("aw", [P, DC], F32)
        sc = sb("sc", [P, 2, DC], F32)
        xm = sb("xm", [P, 2, TT], F32)
        xsc = sb("xsc", [P, 2, TT], F32)
        inv = sb("inv", [P, 2, TT], F32)
        T = ctx.enter_context(nc.psum_tensor("quant_T", [P, 4, S], F32))
        U = ctx.enter_context(nc.psum_tensor("quant_U", [P, 4, S], F32))

        pool_made = sem("pool_made")
        x_in = sem("x_in")
        w_in = sem("w_in")
        c_in = sem("c_in")
        dve_link = sem("dve_link")
        var_ready = sem("var_ready")
        std_ready = sem("std_ready")
        rstd_ready = sem("rstd_ready")
        xn_ready = sem("xn_ready")
        xT_ready = sem("xT_ready")
        wT_ready = sem("wT_ready")
        ax_ready = sem("ax_ready")
        ratio_ready = sem("ratio_ready")
        s_ready = sem("s_ready")
        diag_ready = sem("diag_ready")
        rows_ready = sem("rows_ready")
        ws_ready = sem("ws_ready")
        wdiag_ready = sem("wdiag_ready")
        wrow_ready = sem("wrow_ready")
        wrow_copied = sem("wrow_copied")
        shifted = sem("shifted")
        xq_ready = sem("xq_ready")
        wq_ready = sem("wq_ready")
        xqT_ready = sem("xqT_ready")
        wqT_ready = sem("wqT_ready")
        xqT_copied = sem("xqT_copied")
        wqT_copied = sem("wqT_copied")
        out_ready = sem("out_ready")
        h_ready = sem("h_ready")
        silu_ready = sem("silu_ready")
        a_ready = sem("a_ready")
        x1_ready = sem("x1_ready")
        x1_out = sem("x1_out")

        block = ctx.enter_context(nc.Block())

        @block.gpsimd
        def _(pool):
            nc.gpsimd.memset(ident[:, :], 0.0).then_inc(pool_made, 1)
            nc.gpsimd.memset(identb[:, :], 0.0).then_inc(pool_made, 1)
            nc.gpsimd.memset(ones[:, :], 1.0).then_inc(pool_made, 1)
            nc.gpsimd.memset(eps[:, :], EPS).then_inc(pool_made, 1)
            nc.gpsimd.memset(magic[:, :], MAGIC).then_inc(pool_made, 1)
            pool.wait_ge(pool_made, 5)
            for m in (ident, identb):
                nc.gpsimd.affine_select(out=m[:, :], in_=m[:, :], compare_op=ALU.not_equal, fill=1.0, base=0,
                                        pattern=[[-1, P]], channel_multiplier=1).then_inc(pool_made, 1)

        @block.sync
        def _(sp):
            sp.dma_start(xt[:, :, :], d["x"][0].rearrange("(t p) n -> p t n", p=P)).then_inc(x_in, 16)
            sp.dma_start(wt[:, :, :], d["fw"][0].rearrange("(t p) n -> p t n", p=P)).then_inc(w_in, 16)
            sp.dma_start(ct[:, :, :], d["ctx"][0].rearrange("(t p) n -> p t n", p=P)).then_inc(c_in, 16)
            for b in range(NB):
                if b + 1 < NB:
                    sp.wait_ge(ws_ready, 2 * b + 1)
                    sp.dma_start(wt[:, :, :], d["fw"][b + 1].rearrange("(t p) n -> p t n", p=P)).then_inc(w_in, 16)
                    sp.wait_ge(ws_ready, 2 * b + 2)
                    sp.dma_start(ct[:, :, :], d["ctx"][b + 1].rearrange("(t p) n -> p t n", p=P)).then_inc(c_in, 16)
                sp.wait_ge(x1_ready, b + 1)
                if b + 1 < NB:
                    sp.dma_start(xt[:, :, :], d["x"][b + 1].rearrange("(t p) n -> p t n", p=P)).then_inc(x_in, 16)
                sp.dma_start(s["X1"][b].rearrange("(t p) n -> p t n", p=P), xo[:, :, :]).then_inc(x1_out, 16)
            sp.wait_ge(x1_out, 16 * NB)

        def linears():
            for b in range(NB):
                for lin in range(2):
                    n = 2 * b + lin
                    x, w, nd = ((xn, wt, DC), (a, ct, GU // P))[lin]
                    yield b, lin, n, x, w, nd

        @block.tensor
        def _(pe):
            pe.wait_ge(pool_made, 7)
            for b, lin, n, x, w, nd in linears():
                if lin == 0:
                    pe.wait_ge(xn_ready, TT * b + TT)
                    pe.wait_ge(w_in, 16 * b + 16)
                else:
                    pe.wait_ge(a_ready, b + 1)
                    pe.wait_ge(c_in, 16 * b + 16)
                if n > 0:
                    pe.wait_ge(h_ready, TT * n)
                for c in range(nd):
                    for t in range(TT):
                        last = nc.tensor.transpose(T[:, c, t * P:(t + 1) * P], x[:, t, c * P:(c + 1) * P], ident[:, :])
                last.then_inc(xT_ready, 1)
                for c in range(nd):
                    for t in range(TT):
                        last = nc.tensor.transpose(U[:, c, t * P:(t + 1) * P], w[:, t, c * P:(c + 1) * P], ident[:, :])
                last.then_inc(wT_ready, 1)
                pe.wait_ge(diag_ready, 2 * n + 2)
                for q in range(2):
                    for c in range(nd):
                        last = nc.tensor.matmul(T[:, q, c * P:(c + 1) * P], ones[:, :], dg[:, q, c, :],
                                                start=True, stop=True)
                last.then_inc(rows_ready, 1)
                pe.wait_ge(wdiag_ready, n + 1)
                for c in range(TT):
                    last = nc.tensor.matmul(T[:, 2, c * P:(c + 1) * P], ones[:, :], dg[:, 2, c, :], start=True, stop=True)
                last.then_inc(wrow_ready, 1)
                pe.wait_ge(wrow_copied, n + 1)
                pe.wait_ge(xq_ready, n + 1)
                for c in range(nd):
                    for t in range(TT):
                        last = nc.tensor.transpose(T[:, c, 0:S // 2].bitcast(BF16)[:, t * P:(t + 1) * P],
                                                   xq[:, t, c * P:(c + 1) * P], identb[:, :])
                last.then_inc(xqT_ready, 1)
                pe.wait_ge(wq_ready, n + 1)
                for c in range(nd):
                    for t in range(TT):
                        last = nc.tensor.transpose(U[:, c, 0:S // 2].bitcast(BF16)[:, t * P:(t + 1) * P],
                                                   wq[:, t, c * P:(c + 1) * P], identb[:, :])
                last.then_inc(wqT_ready, 1)
                pe.wait_ge(xqT_copied, n + 1)
                pe.wait_ge(wqT_copied, n + 1)
                for t in range(TT):
                    for c in range(nd):
                        last = nc.tensor.matmul(U[:, t, :], xqT[:, c, t * P:(t + 1) * P], wqT[:, c, :],
                                                start=(c == 0), stop=(c == nd - 1))
                    last.then_inc(out_ready, 1)

        @block.scalar
        def _(act):
            act.wait_ge(pool_made, 7)
            for b, lin, n, x, w, nd in linears():
                if lin == 0:
                    act.wait_ge(var_ready, TT * b + TT)
                    nc.scalar.activation(rstd[:, :], mv[:, :, 1], ACT.Sqrt, bias=eps[:, :]).then_inc(std_ready, 1)
                    act.wait_ge(rstd_ready, b + 1)
                    for t in range(TT):
                        nc.scalar.activation(xn[:, t, :], xt[:, t, :], ACT.Identity, bias=nmr[:, t:t + 1],
                                             scale=rstd[:, t:t + 1]).then_inc(xn_ready, 1)
                act.wait_ge(ratio_ready, n + 1)
                nc.scalar.activation(sc[:, 1, 0:nd], sc[:, 0, 0:nd], ACT.Sqrt).then_inc(s_ready, 1)
                act.wait_ge(wrow_ready, n + 1)
                nc.scalar.activation(wscB[:, :], T[:, 2, :], ACT.Copy).then_inc(wrow_copied, 1)
                for q, r in enumerate((xs, ws)):
                    for t in range(TT):
                        nc.scalar.activation(r[:, t, 0:nd * P], r[:, t, 0:nd * P], ACT.Identity, bias=magic[:, :],
                                             scale=inv[:, q, t:t + 1]).then_inc(shifted, 1)
                act.wait_ge(xqT_ready, n + 1)
                nc.scalar.activation(xqT[:, 0:nd, :], T[:, 0:nd, 0:S // 2].bitcast(BF16), ACT.Copy).then_inc(xqT_copied, 1)
                if lin == 0:
                    act.wait_ge(h_ready, TT * n + TT)
                    nc.scalar.activation(sg[:, :, :], h[:, :, 0:GU], ACT.Silu).then_inc(silu_ready, 1)

        @block.vector
        def _(dve):
            dve.wait_ge(pool_made, 7)
            link = Link(dve, dve_link)
            for b, lin, n, x, w, nd in linears():
                W = nd * P
                if lin == 0:
                    dve.wait_ge(x_in, 16 * b + 16)
                    for t in range(TT):
                        link(nc.vector.bn_stats(stats[:, t, :], xt[:, t, :]))
                    for t in range(TT):
                        nc.vector.bn_aggr(mv[:, t, :], stats[:, t, :]).then_inc(var_ready, 1)
                    dve.wait_ge(std_ready, b + 1)
                    link(nc.vector.reciprocal(rstd[:, :], rstd[:, :]))
                    nc.vector.scalar_tensor_tensor(out=nmr[:, :], in0=mv[:, :, 0], scalar=-1.0, in1=rstd[:, :],
                                                   op0=ALU.mult, op1=ALU.mult).then_inc(rstd_ready, 1)
                for m, ps, ready in ((ax, T, xT_ready), (aw, U, wT_ready)):
                    dve.wait_ge(ready, n + 1)
                    link(nc.vector.tensor_reduce(m[:, 0:nd], ps[:, 0:nd, :], AX_X, ALU.max, apply_absolute_value=True))
                    link(nc.vector.tensor_scalar(m[:, 0:nd], m[:, 0:nd], QEPS, None, ALU.max))
                link(nc.vector.reciprocal(aw[:, 0:nd], aw[:, 0:nd]))
                nc.vector.tensor_tensor(sc[:, 0, 0:nd], ax[:, 0:nd], aw[:, 0:nd], ALU.mult).then_inc(ratio_ready, 1)
                dve.wait_ge(s_ready, n + 1)
                link(nc.vector.tensor_scalar(sc[:, 1, 0:nd], sc[:, 1, 0:nd], QEPS, None, ALU.max))
                link(nc.vector.reciprocal(sc[:, 0, 0:nd], sc[:, 1, 0:nd]))
                for q in range(2):
                    nc.vector.tensor_tensor(dg[:, q, 0:nd, :], ident[:, :].unsqueeze(1).to_broadcast([P, nd, P]),
                                            sc[:, q, 0:nd].unsqueeze(2).to_broadcast([P, nd, P]),
                                            ALU.mult).then_inc(diag_ready, 1)
                dve.wait_ge(rows_ready, n + 1)
                nc.vector.tensor_tensor(ws[:, :, 0:W], w[:, :, 0:W], T[:, 1, 0:W].unsqueeze(1).to_broadcast([P, TT, W]),
                                        ALU.mult).then_inc(ws_ready, 1)
                link(nc.vector.tensor_tensor(xs[:, :, 0:W], x[:, :, 0:W],
                                             T[:, 0, 0:W].unsqueeze(1).to_broadcast([P, TT, W]), ALU.mult))
                dve.wait_ge(ws_ready, n + 1)
                link(nc.vector.tensor_reduce(xm[:, 1, :], ws[:, :, 0:W], AX_X, ALU.max, apply_absolute_value=True))
                link(nc.vector.tensor_reduce(xm[:, 0, :], xs[:, :, 0:W], AX_X, ALU.max, apply_absolute_value=True))
                link(nc.vector.tensor_scalar(xsc[:, :, :], xm[:, :, :], QEPS, 1.0 / QMAX, ALU.max, ALU.mult))
                link(nc.vector.reciprocal(inv[:, :, :], xsc[:, :, :]))
                nc.vector.tensor_tensor(dg[:, 2, :, :], ident[:, :].unsqueeze(1).to_broadcast([P, TT, P]),
                                        xsc[:, 1, :].unsqueeze(2).to_broadcast([P, TT, P]), ALU.mult).then_inc(wdiag_ready, 1)
                for q, (r, o, ready) in enumerate(((xs, xq, xq_ready), (ws, wq, wq_ready))):
                    dve.wait_ge(shifted, 2 * TT * n + TT * (q + 1))
                    link(nc.vector.tensor_scalar(o[:, :, 0:W], r[:, :, 0:W], MAGIC, QMAX, ALU.subtract, ALU.min))
                    nc.vector.tensor_scalar(o[:, :, 0:W], o[:, :, 0:W], -QMAX, None, ALU.max).then_inc(ready, 1)
                dve.wait_ge(wqT_ready, n + 1)
                nc.vector.tensor_copy(wqT[:, 0:nd, :], U[:, 0:nd, 0:S // 2].bitcast(BF16)).then_inc(wqT_copied, 1)
                for t in range(TT):
                    dve.wait_ge(out_ready, TT * n + t + 1)
                    dve.wait_ge(wrow_copied, n + 1)
                    nc.vector.scalar_tensor_tensor(out=h[:, t, :], in0=U[:, t, :], scalar=xsc[:, 0, t:t + 1],
                                                   in1=wscB[:, :], op0=ALU.mult, op1=ALU.mult).then_inc(h_ready, 1)
                dve.wait_ge(h_ready, TT * n + TT)
                if lin == 0:
                    dve.wait_ge(silu_ready, b + 1)
                    nc.vector.tensor_tensor(a[:, :, :], sg[:, :, :], h[:, :, GU:2 * GU], ALU.mult).then_inc(a_ready, 1)
                    dve.wait_ge(a_ready, b + 1)
                else:
                    if b > 0:
                        dve.wait_ge(x1_out, 16 * b)
                    nc.vector.tensor_tensor(xo[:, :, :], xt[:, :, :], h[:, :, :], ALU.add).then_inc(x1_ready, 1)


NG = 4
UNITS = (NST // NG) * DC
WBUF = 3


def mix_block(nc, d, s):
    with ExitStack() as ctx:
        sems = []

        def sb(name, shape, dt):
            return ctx.enter_context(nc.sbuf_tensor("mix_" + name, shape, dt))

        def sem(name):
            sems.append(ctx.enter_context(nc.semaphore("mix_" + name)))
            return sems[-1]

        ident = sb("ident", [P, P], F32)
        eps = sb("eps_col", [P, 1], F32)
        fence = sb("fence", [P, 1], F32)
        A = sb("A", [P, DC, NST], F32)
        dskip = sb("dskip", [P, DC], F32)
        xt = sb("xt", [P, TT, D], F32)
        xn = sb("xn", [P, TT, D], F32)
        xo = sb("xo", [P, TT, D], F32)
        xThi = sb("xThi", [P, DC, S], F32R)
        xTlo = sb("xTlo", [P, DC, S], F32R)
        stats = sb("stats", [P, TT, 6], F32)
        mv = sb("mv", [P, TT, 2], F32)
        rstd = sb("rstd", [P, TT], F32)
        nmr = sb("nmr", [P, TT], F32)
        w = sb("w", [P, WBUF, 2 * WCH], F32R)
        th = sb("th", [P, 2, S], F32)
        hf = sb("hf", [P, 2, S], F32)
        hhi = sb("hhi", [P, 2, S], F32R)
        hlo = sb("hlo", [P, 2, S], F32R)
        dt = sb("dt", [P, DC, S], F32)
        du = sb("du", [P, DC, S], F32)
        u = sb("u", [P, DC, S], F32)
        y = sb("y", [P, DC, S], F32)
        Bb = sb("Bb", [P, 2, NG, S], F32)
        Cb = sb("Cb", [P, 2, NG, S], F32)
        dA = sb("dA", [P, 2, NG, S], F32)
        st = sb("st", [P, 2, NG, S], F32)
        G = ctx.enter_context(nc.psum_tensor("mix_G", [P, 2, 2, S], F32))
        Dp = ctx.enter_context(nc.psum_tensor("mix_Dp", [P, TT, S], F32))

        const_in = sem("const_in")
        pool_made = sem("pool_made")
        x_in = sem("x_in")
        proj_in = sem("proj_in")
        w_in = [sem(f"w_in{i}") for i in range(WBUF)]
        bc_in = [sem(f"bc_in{i}") for i in range(2)]
        a_made = sem("a_made")
        dve_link = sem("dve_link")
        var_ready = sem("var_ready")
        std_ready = sem("std_ready")
        rstd_ready = sem("rstd_ready")
        xn_ready = sem("xn_ready")
        xT_ready = sem("xT_ready")
        hi_ready = sem("hi_ready")
        lo_ready = sem("lo_ready")
        gu_ready = sem("gu_ready")
        tanh_ready = sem("tanh_ready")
        h_ready = sem("h_ready")
        hhi_ready = sem("hhi_ready")
        hlo_ready = sem("hlo_ready")
        chunk_done = sem("chunk_done")
        da_ready = sem("da_ready")
        dbu_ready = sem("dbu_ready")
        unit_done = sem("unit_done")
        x2_ready = sem("x2_ready")
        z_ready = sem("z_ready")
        gated = sem("gated")
        gT_ready = sem("gT_ready")
        x3_ready = sem("x3_ready")
        x3_out = sem("x3_out")
        start_at_one(nc, sems)
        block = ctx.enter_context(nc.Block())

        SLOT = [j * UNITS // CH for j in range(CH)]

        @block.gpsimd
        def _(pool):
            nc.gpsimd.memset(eps[:, :], EPS).then_inc(pool_made, 1)
            nc.gpsimd.memset(ident[:, :], 0.0).then_inc(pool_made, 1)
            nc.gpsimd.memset(dA[:, :, :, 0:1], 0.0).then_inc(pool_made, 1)
            need(pool, pool_made, 3)
            nc.gpsimd.affine_select(out=ident[:, :], in_=ident[:, :], compare_op=ALU.not_equal, fill=1.0, base=0,
                                    pattern=[[-1, P]], channel_multiplier=1).then_inc(pool_made, 1)
            with pool.Fori(0, NB) as b:
                def low_half(j):
                    need(pool, hhi_ready, CH * b + j + 1)
                    need(pool, chunk_done, CH * b + max(j - 1, 0))
                    nc.gpsimd.tensor_tensor(hlo[:, j % 2, :], hf[:, j % 2, :], hhi[:, j % 2, :].bitcast(F32),
                                            ALU.subtract).then_inc(hlo_ready, 1)

                need(pool, proj_in, 48 * b + 48)
                for k in range(UNITS):
                    ng, c = divmod(k, DC)
                    if k % DC == 0:
                        need(pool, bc_in[ng % 2], 32 * (NST // NG // 2) * b + 32 * (ng // 2 + 1))
                    need(pool, unit_done, UNITS * b + max(k - 1, 0))
                    nc.gpsimd.tensor_tensor(st[:, k % 2, :, :], Bb[:, ng % 2, :, :],
                                            du[:, c, :].unsqueeze(1).to_broadcast([P, NG, S]),
                                            ALU.mult).then_inc(dbu_ready, 1)
                    for j in range(CH):
                        if SLOT[j] == k:
                            low_half(j)

        @block.sync
        def _(sp):
            sp.dma_start(A[:, :, :], d["alog"]).then_inc(const_in, 16)
            sp.dma_start(dskip[:, :], d["dskip"]).then_inc(const_in, 16)
            with sp.Fori(0, NB) as b:
                def load_w(j):
                    need(sp, chunk_done, CH * b + max(j - WBUF + 1, 0))
                    sp.dma_start(w[:, j % WBUF, :].bitcast(F32), s["W"][j]).then_inc(w_in[j % WBUF], 16)

                def load_bc(ng):
                    need(sp, unit_done, UNITS * b + max(DC * (ng - 1), 0))
                    for dst, at in ((Bb, 0), (Cb, NST)):
                        sp.dma_start(dst[:, ng % 2, :, :],
                                     s["BC"][b][at + NG * ng:at + NG * ng + NG, :].unsqueeze(0).to_broadcast([P, NG, S])
                                     ).then_inc(bc_in[ng % 2], 16)

                need(sp, x3_ready, b)
                sp.dma_start(xt[:, :, :], s["X1"][b].rearrange("(t p) n -> p t n", p=P)).then_inc(x_in, 16)
                for dst, name in ((dt, "DT"), (du, "DU"), (u, "U")):
                    sp.dma_start(dst[:, :, :], s[name][b]).then_inc(proj_in, 16)
                load_bc(0)
                for j in range(WBUF):
                    load_w(j)
                load_bc(1)
                for j in range(WBUF, CH):
                    load_w(j)
                    if j in (6, 9):
                        load_bc(2 if j == 6 else 3)
                need(sp, x3_ready, b + 1)
                sp.dma_start(s["X3"][b].rearrange("(t p) n -> p t n", p=P), xo[:, :, :]).then_inc(x3_out, 16)
            need(sp, x3_out, 16 * NB)

        @block.tensor
        def _(pe):
            need(pe, pool_made, 4)
            with pe.Fori(0, NB) as b:
                need(pe, xn_ready, 2 * TT * b + TT)
                need(pe, x3_ready, b)
                for c in range(DC):
                    for t in range(TT):
                        last = nc.tensor.transpose(Dp[:, c, t * P:(t + 1) * P], xn[:, t, c * P:(c + 1) * P], ident[:, :])
                last.then_inc(xT_ready, 1)
                need(pe, hi_ready, b + 1)
                need(pe, lo_ready, b + 1)

                def up(j):
                    need(pe, w_in[j % WBUF], 16 * len(range(j % WBUF, CH, WBUF)) * b + 16 * (j // WBUF + 1))
                    need(pe, h_ready, CH * b + max(j - 1, 0))
                    wb = w[:, j % WBUF, :]
                    for q in range(2):
                        steps = [(c, x, at) for c in range(DC) for x, at in ((xThi, 0), (xTlo, 0), (xThi, WCH))]
                        for i, (c, x, at) in enumerate(steps):
                            col = at + q * D + c * P
                            last = nc.tensor.matmul(G[:, j % 2, q, :], wb[:, col:col + P], x[:, c, :],
                                                    start=(i == 0), stop=(i == len(steps) - 1))
                    last.then_inc(gu_ready, 1)

                def down(j):
                    need(pe, hlo_ready, CH * b + j + 1)
                    n = P if j < CH - 1 else LAST
                    wb = w[:, j % WBUF, :]
                    for t in range(TT):
                        for i, (h, at) in enumerate(((hhi, 0), (hhi, WCH), (hlo, 0))):
                            last = nc.tensor.matmul(Dp[:, t, :], h[0:n, j % 2, t * P:(t + 1) * P],
                                                    wb[0:n, at + 2 * D:at + 3 * D],
                                                    start=(j == 0 and i == 0), stop=(j == CH - 1 and i == 2))
                    last.then_inc(chunk_done, 1)

                up(0)
                for j in range(CH):
                    if j + 1 < CH:
                        up(j + 1)
                    down(j)
                need(pe, gated, b + 1)
                for t in range(TT):
                    for c in range(DC):
                        last = nc.tensor.transpose(Dp[:, t, c * P:(c + 1) * P], y[:, c, t * P:(t + 1) * P], ident[:, :])
                last.then_inc(gT_ready, 1)

        @block.scalar
        def _(act):
            need(act, const_in, 32)
            need(act, pool_made, 4)
            nc.scalar.activation(A[:, :, :], A[:, :, :], ACT.Exp).then_inc(a_made, 1)
            need(act, a_made, 1)
            nc.scalar.mul(A[:, :, :], A[:, :, :], -1.0).then_inc(a_made, 1)
            need(act, a_made, 2)

            def normalise(n):
                need(act, var_ready, n + 1)
                nc.scalar.activation(rstd[:, :], mv[:, :, 1], ACT.Sqrt, bias=eps[:, :]).then_inc(std_ready, 1)
                need(act, rstd_ready, n + 1)
                for t in range(TT):
                    nc.scalar.activation(xn[:, t, :], xt[:, t, :], ACT.Identity, bias=nmr[:, t:t + 1],
                                         scale=rstd[:, t:t + 1]).then_inc(xn_ready, 1)

            with act.Fori(0, NB) as b:
                def tanh(j):
                    need(act, gu_ready, CH * b + j + 1)
                    need(act, h_ready, CH * b + max(j - 1, 0))
                    nc.scalar.activation(th[:, j % 2, :], G[:, j % 2, 0, :], ACT.Tanh, scale=0.5).then_inc(tanh_ready, 1)

                def high_half(j):
                    need(act, h_ready, CH * b + j + 1)
                    need(act, chunk_done, CH * b + max(j - 1, 0))
                    nc.scalar.activation(hhi[:, j % 2, :], hf[:, j % 2, :], ACT.Copy).then_inc(hhi_ready, 1)

                need(act, gated, b)
                normalise(2 * b)
                need(act, xT_ready, b + 1)
                nc.scalar.activation(xThi[:, :, :], Dp[:, :, :], ACT.Copy).then_inc(hi_ready, 1)
                need(act, proj_in, 48 * b + 48)
                for k in range(UNITS):
                    ng, c = divmod(k, DC)
                    for j in range(CH):
                        if SLOT[j] == k:
                            tanh(j)
                    need(act, unit_done, UNITS * b + max(k - 1, 0))
                    for n in range(NG):
                        m = NG * ng + n
                        last = nc.scalar.activation(dA[:, k % 2, n, 1:S], dt[:, c, 1:S], ACT.Exp, scale=A[:, c, m:m + 1])
                    last.then_inc(da_ready, 1)
                    for j in range(CH):
                        if SLOT[j] == k:
                            high_half(j)
                normalise(2 * b + 1)
                need(act, xn_ready, 2 * TT * b + 2 * TT)
                nc.scalar.activation(xn[:, :, :], xn[:, :, :], ACT.Silu).then_inc(z_ready, 1)

        @block.vector
        def _(dve):
            LINKS = 2 * (TT + 1) + (UNITS - DC) * 4 + DC * 3 + CH + DC
            need(dve, pool_made, 4)
            with dve.Fori(0, NB) as b:
                link = Link(dve, dve_link, b * LINKS + 1)

                def moments(n):
                    for t in range(TT):
                        link(nc.vector.bn_stats(stats[:, t, :], xt[:, t, :]))
                    nc.vector.memset(fence[:, :], 0.0)
                    for t in range(TT):
                        last = nc.vector.bn_aggr(mv[:, t, :], stats[:, t, :])
                    last.then_inc(var_ready, 1)
                    need(dve, std_ready, n + 1)
                    link(nc.vector.reciprocal(rstd[:, :], rstd[:, :]))
                    nc.vector.scalar_tensor_tensor(out=nmr[:, :], in0=mv[:, :, 0], scalar=-1.0, in1=rstd[:, :],
                                                   op0=ALU.mult, op1=ALU.mult).then_inc(rstd_ready, 1)

                def hidden(j):
                    need(dve, tanh_ready, CH * b + j + 1)
                    link(nc.vector.scalar_tensor_tensor(out=th[:, j % 2, :], in0=th[:, j % 2, :], scalar=1.0,
                                                        in1=G[:, j % 2, 0, :], op0=ALU.add, op1=ALU.mult))
                    need(dve, hlo_ready, CH * b + max(j - 1, 0))
                    nc.vector.scalar_tensor_tensor(out=hf[:, j % 2, :], in0=th[:, j % 2, :], scalar=0.5,
                                                   in1=G[:, j % 2, 1, :], op0=ALU.mult, op1=ALU.mult).then_inc(h_ready, 1)

                need(dve, x_in, 16 * b + 16)
                moments(2 * b)
                need(dve, hi_ready, b + 1)
                nc.vector.tensor_tensor(xTlo[:, :, :], Dp[:, :, :], xThi[:, :, :].bitcast(F32),
                                        ALU.subtract).then_inc(lo_ready, 1)
                for k in range(UNITS):
                    ng, c = divmod(k, DC)
                    r = st[:, k % 2, :, :]
                    for j in range(CH):
                        if SLOT[j] == k:
                            hidden(j)
                    need(dve, da_ready, UNITS * b + k + 1)
                    need(dve, dbu_ready, UNITS * b + k + 1)
                    flat = r.rearrange("p n s -> p (n s)")
                    link(nc.vector.tensor_tensor_scan(flat, dA[:, k % 2, :, :].rearrange("p n s -> p (n s)"), flat, 0.0,
                                                      ALU.mult, ALU.add))
                    need(dve, bc_in[ng % 2], 32 * (NST // NG // 2) * b + 32 * (ng // 2 + 1))
                    link(nc.vector.tensor_tensor(r, r, Cb[:, ng % 2, :, :], ALU.mult))
                    link(nc.vector.tensor_tensor(r[:, 0:2, :], r[:, 0:2, :], r[:, 2:4, :], ALU.add))
                    if ng == 0:
                        nc.vector.tensor_tensor(y[:, c, :], r[:, 0, :], r[:, 1, :], ALU.add).then_inc(unit_done, 1)
                    else:
                        link(nc.vector.tensor_tensor(r[:, 0, :], r[:, 0, :], r[:, 1, :], ALU.add))
                        nc.vector.tensor_tensor(y[:, c, :], y[:, c, :], r[:, 0, :], ALU.add).then_inc(unit_done, 1)
                need(dve, unit_done, UNITS * b + UNITS)
                need(dve, chunk_done, CH * b + CH)
                nc.vector.tensor_tensor(xt[:, :, :], xt[:, :, :], Dp[:, :, :], ALU.add).then_inc(x2_ready, 1)
                need(dve, x2_ready, b + 1)
                moments(2 * b + 1)
                for c in range(DC):
                    link(nc.vector.scalar_tensor_tensor(out=y[:, c, :], in0=u[:, c, :], scalar=dskip[:, c:c + 1],
                                                        in1=y[:, c, :], op0=ALU.mult, op1=ALU.add))
                need(dve, z_ready, b + 1)
                nc.vector.tensor_tensor(y[:, :, :], y[:, :, :], xn[:, :, :], ALU.mult).then_inc(gated, 1)
                need(dve, gT_ready, b + 1)
                need(dve, x3_out, 16 * b)
                nc.vector.tensor_tensor(xo[:, :, :], xt[:, :, :], Dp[:, :, :], ALU.add).then_inc(x3_ready, 1)
                assert link.n == LINKS, (link.n, LINKS)


E_N = 32
F = 192
F2 = F - P
TOP = 8
TILES = NB * TT
CAP = 2 * (NB * S * TOP // E_N)
GUC = 3 * P
EW = DC * GUC


def route_block(nc, d, s, X, xThi, xTlo, wts):
    with ExitStack() as ctx:
        def sb(name, shape, dt):
            return ctx.enter_context(nc.sbuf_tensor("route_" + name, shape, dt))

        def sem(name):
            return ctx.enter_context(nc.semaphore("route_" + name))

        ident = sb("ident", [P, P], F32)
        onesb = sb("onesb", [P, P], BF16)
        tri = sb("tri", [P, P], BF16)
        eps = sb("eps_col", [P, 1], F32)
        gw = sb("gw", [P, DC, E_N], F32)
        gwhi = sb("gwhi", [P, DC, E_N], F32R)
        gwlo = sb("gwlo", [P, DC, E_N], F32R)
        xn = sb("xn", [P, 2, TT, D], F32)
        stats = sb("stats", [P, TT, 6], F32)
        mv = sb("mv", [P, TT, 2], F32)
        rstd = sb("rstd", [P, TT], F32)
        nmr = sb("nmr", [P, TT], F32)
        pr = sb("pr", [P, TILES, E_N], F32)
        rest = sb("rest", [P, TILES, E_N], F32)
        mask = sb("mask", [P, TILES, E_N], BF16)
        before = sb("before", [P, TILES, E_N], BF16)
        mx = sb("mx", [P, TILES], F32)
        top = sb("top", [P, TILES, TOP], F32)
        T = ctx.enter_context(nc.psum_tensor("route_T", [P, DC, S], F32))
        L = ctx.enter_context(nc.psum_tensor("route_L", [P, TILES, E_N], F32))
        R = ctx.enter_context(nc.psum_tensor("route_R", [P, TILES, E_N], F32))

        x_in = [sem(f"x_in{b}") for b in range(NB)]
        g_in = sem("g_in")
        pool_made = sem("pool_made")
        dve_link = sem("dve_link")
        gw_split = sem("gw_split")
        var_ready = sem("var_ready")
        std_ready = sem("std_ready")
        rstd_ready = sem("rstd_ready")
        xn_ready = sem("xn_ready")
        xT_ready = sem("xT_ready")
        hi_ready = sem("hi_ready")
        lo_ready = sem("lo_ready")
        logits_ready = sem("logits_ready")
        shifted = sem("shifted")
        exp_ready = sem("exp_ready")
        mask_ready = sem("mask_ready")
        before_ready = sem("before_ready")
        rank_ready = sem("rank_ready")

        block = ctx.enter_context(nc.Block())

        @block.sync
        def _(sp):
            for b in range(NB):
                sp.dma_start(X[:, b * TT:(b + 1) * TT, :], s["X3"][b].rearrange("(t p) n -> p t n", p=P)).then_inc(x_in[b], 16)
            sp.dma_start(gw[:, :, :], d["gw"].rearrange("(c p) e -> p c e", p=P)).then_inc(g_in, 16)

        @block.gpsimd
        def _(pool):
            nc.gpsimd.memset(ident[:, :], 0.0).then_inc(pool_made, 1)
            nc.gpsimd.memset(onesb[:, :], 1.0).then_inc(pool_made, 1)
            nc.gpsimd.memset(tri[:, :], 1.0).then_inc(pool_made, 1)
            nc.gpsimd.memset(eps[:, :], EPS).then_inc(pool_made, 1)
            pool.wait_ge(pool_made, 4)
            nc.gpsimd.affine_select(out=ident[:, :], in_=ident[:, :], compare_op=ALU.not_equal, fill=1.0, base=0,
                                    pattern=[[-1, P]], channel_multiplier=1).then_inc(pool_made, 1)
            nc.gpsimd.affine_select(out=tri[:, :], in_=tri[:, :], compare_op=ALU.is_gt, fill=0.0, base=0,
                                    pattern=[[1, P]], channel_multiplier=-1).then_inc(pool_made, 1)

        @block.tensor
        def _(pe):
            pe.wait_ge(pool_made, 6)
            pe.wait_ge(gw_split, 2)
            for b in range(NB):
                pe.wait_ge(xn_ready, TT * b + TT)
                if b > 0:
                    pe.wait_ge(lo_ready, b)
                for c in range(DC):
                    for t in range(TT):
                        last = nc.tensor.transpose(T[:, c, t * P:(t + 1) * P], xn[:, b % 2, t, c * P:(c + 1) * P], ident[:, :])
                last.then_inc(xT_ready, 1)
                pe.wait_ge(hi_ready, b + 1)
                pe.wait_ge(lo_ready, b + 1)
                for t in range(TT):
                    cols = slice(b * S + t * P, b * S + (t + 1) * P)
                    steps = [(c, x, g) for c in range(DC) for x, g in ((xThi, gwhi), (xTlo, gwhi), (xThi, gwlo))]
                    for i, (c, x, g) in enumerate(steps):
                        last = nc.tensor.matmul(L[:, b * TT + t, :], x[:, c, cols], g[:, c, :],
                                                start=(i == 0), stop=(i == len(steps) - 1))
                last.then_inc(logits_ready, 1)
            pe.wait_ge(mask_ready, 1)
            pe.wait_ge(before_ready, TILES - 1)
            for i in range(TILES):
                last = nc.tensor.matmul(R[:, i, :], tri[:, :], mask[:, i, :], start=True, stop=(i == 0))
                if i > 0:
                    last = nc.tensor.matmul(R[:, i, :], onesb[:, :], before[:, i, :], start=False, stop=True)
            last.then_inc(rank_ready, 1)

        @block.scalar
        def _(act):
            act.wait_ge(pool_made, 6)
            for b in range(NB):
                act.wait_ge(var_ready, TT * b + TT)
                nc.scalar.activation(rstd[:, :], mv[:, :, 1], ACT.Sqrt, bias=eps[:, :]).then_inc(std_ready, 1)
                act.wait_ge(rstd_ready, b + 1)
                if b >= 2:
                    act.wait_ge(xT_ready, b - 1)
                for t in range(TT):
                    nc.scalar.activation(xn[:, b % 2, t, :], X[:, b * TT + t, :], ACT.Identity, bias=nmr[:, t:t + 1],
                                         scale=rstd[:, t:t + 1]).then_inc(xn_ready, 1)
                act.wait_ge(xT_ready, b + 1)
                nc.scalar.activation(xThi[:, :, b * S:(b + 1) * S], T[:, :, :], ACT.Copy).then_inc(hi_ready, 1)
            act.wait_ge(shifted, 1)
            nc.scalar.activation(pr[:, :, :], pr[:, :, :], ACT.Exp).then_inc(exp_ready, 1)

        @block.vector
        def _(dve):
            link = Link(dve, dve_link)
            dve.wait_ge(g_in, 16)
            nc.vector.tensor_copy(gwhi[:, :, :], gw[:, :, :]).then_inc(gw_split, 1)
            dve.wait_ge(gw_split, 1)
            nc.vector.tensor_tensor(gwlo[:, :, :], gw[:, :, :], gwhi[:, :, :].bitcast(F32), ALU.subtract).then_inc(gw_split, 1)
            for b in range(NB):
                dve.wait_ge(x_in[b], 16)
                for t in range(TT):
                    link(nc.vector.bn_stats(stats[:, t, :], X[:, b * TT + t, :]))
                if b > 0:
                    dve.wait_ge(xn_ready, TT * b)
                for t in range(TT):
                    nc.vector.bn_aggr(mv[:, t, :], stats[:, t, :]).then_inc(var_ready, 1)
                dve.wait_ge(std_ready, b + 1)
                link(nc.vector.reciprocal(rstd[:, :], rstd[:, :]))
                nc.vector.scalar_tensor_tensor(out=nmr[:, :], in0=mv[:, :, 0], scalar=-1.0, in1=rstd[:, :],
                                               op0=ALU.mult, op1=ALU.mult).then_inc(rstd_ready, 1)
                dve.wait_ge(hi_ready, b + 1)
                nc.vector.tensor_tensor(xTlo[:, :, b * S:(b + 1) * S], T[:, :, :],
                                        xThi[:, :, b * S:(b + 1) * S].bitcast(F32), ALU.subtract).then_inc(lo_ready, 1)
            dve.wait_ge(logits_ready, NB)
            def over(m):
                return m.unsqueeze(2).to_broadcast([P, TILES, E_N])
            link(nc.vector.tensor_reduce(mx[:, :], L[:, :, :], AX_X, ALU.max))
            nc.vector.tensor_tensor(pr[:, :, :], L[:, :, :], over(mx[:, :]), ALU.subtract).then_inc(shifted, 1)
            dve.wait_ge(exp_ready, 1)
            link(nc.vector.tensor_reduce(mx[:, :], pr[:, :, :], AX_X, ALU.add))
            link(nc.vector.reciprocal(mx[:, :], mx[:, :]))
            link(nc.vector.tensor_tensor(pr[:, :, :], pr[:, :, :], over(mx[:, :]), ALU.mult))
            for i in range(TILES):
                link(nc.vector.max(top[:, i, :], pr[:, i, :]))
            for i in range(TILES):
                link(nc.vector.match_replace(rest[:, i, :], top[:, i, :], pr[:, i, :], -1.0))
            nc.vector.tensor_scalar(mask[:, :, :], rest[:, :, :], 0.0, None, ALU.is_lt).then_inc(mask_ready, 1)
            dve.wait_ge(mask_ready, 1)
            for i in range(1, TILES):
                if i == 1:
                    nc.vector.tensor_copy(before[:, 1, :], mask[:, 0, :]).then_inc(before_ready, 1)
                else:
                    nc.vector.tensor_tensor(before[:, i, :], before[:, i - 1, :], mask[:, i - 1, :],
                                            ALU.add).then_inc(before_ready, 1)
                dve.wait_ge(before_ready, i)
            link(nc.vector.tensor_reduce(mx[:, :], top[:, :, :], AX_X, ALU.add))
            link(nc.vector.reciprocal(mx[:, :], mx[:, :]))
            link(nc.vector.tensor_tensor(pr[:, :, :], pr[:, :, :], over(mx[:, :]), ALU.mult))
            link(nc.vector.tensor_tensor(pr[:, :, :], pr[:, :, :], mask[:, :, :], ALU.mult))
            dve.wait_ge(rank_ready, 1)
            link(nc.vector.scalar_tensor_tensor(out=wts[:, :, :], in0=R[:, :, :], scalar=float(CAP), in1=pr[:, :, :],
                                                op0=ALU.is_lt, op1=ALU.mult))


def expert_block(nc, d, out, X, xThi, xTlo, wts):
    with ExitStack() as ctx:
        sems = []

        def sb(name, shape, dt):
            return ctx.enter_context(nc.sbuf_tensor("moe_" + name, shape, dt))

        def sem(name):
            sems.append(ctx.enter_context(nc.semaphore("moe_" + name)))
            return sems[-1]

        raw = sb("raw", [P, EW + 2 * D], F32)
        whi = sb("whi", [P, 2, EW + 2 * D], F32R)
        wlo = sb("wlo", [P, 2, EW + 2 * D], F32R)
        th = sb("th", [P, 2, 2, S], F32)
        hf = sb("hf", [P, 2, 2, S], F32)
        hhi = sb("hhi", [P, 2, 2, S], F32R)
        hlo = sb("hlo", [P, 2, 2, S], F32R)
        wcol = sb("wcol", [P, E_N, TILES], F32)
        G = ctx.enter_context(nc.psum_tensor("moe_G", [P, 3, S], F32))
        Y = ctx.enter_context(nc.psum_tensor("moe_Y", [P, TT, S], F32))

        raw_in = sem("raw_in")
        hi_ready = sem("hi_ready")
        lo_ready = sem("lo_ready")
        gu_ready = sem("gu_ready")
        tanh_ready = sem("tanh_ready")
        dve_link = sem("dve_link")
        h_ready = sem("h_ready")
        hhi_ready = sem("hhi_ready")
        hlo_ready = sem("hlo_ready")
        y_ready = sem("y_ready")
        added = sem("added")
        x_out = sem("x_out")
        start_at_one(nc, sems)
        block = ctx.enter_context(nc.Block())
        PAIR = 2 * NB

        @block.sync
        def _(sp):
            with sp.Fori(0, E_N // 2) as i:
                for q in range(2):
                    need(sp, lo_ready, 2 * i + q)
                    sp.dma_start(raw[:, :], d["ew"][i * 2 + q]).then_inc(raw_in, 16)
            need(sp, added, TT * NB * E_N)
            sp.dma_start(out.rearrange("b (t p) n -> p (b t) n", p=P), X[:, :, :]).then_inc(x_out, 16)
            need(sp, x_out, 16)

        @block.gpsimd
        def _(pool):
            def low_weights(i, q, n):
                need(pool, hi_ready, n + 1)
                need(pool, y_ready, PAIR * i * TT + max(q - 1, 0) * NB * TT)
                nc.gpsimd.tensor_tensor(wlo[:, q, :], raw[:, :], whi[:, q, :].bitcast(F32), ALU.subtract).then_inc(lo_ready, 1)

            with pool.Fori(0, E_N // 2) as i:
                for q in range(2):
                    low_weights(i, q, i * 2 + q)
                    for g in range(NB):
                        need(pool, hhi_ready, 2 * (PAIR * i + NB * q + g + 1))
                        need(pool, y_ready, TT * (PAIR * i + NB * q + max(g - 1, 0)))
                        nc.gpsimd.tensor_tensor(hlo[:, g % 2, 0, :], hf[:, g % 2, 0, :], hhi[:, g % 2, 0, :].bitcast(F32),
                                                ALU.subtract).then_inc(hlo_ready, 1)
                        nc.gpsimd.tensor_tensor(hlo[0:F2, g % 2, 1, :], hf[0:F2, g % 2, 1, :],
                                                hhi[0:F2, g % 2, 1, :].bitcast(F32), ALU.subtract).then_inc(hlo_ready, 1)

        @block.scalar
        def _(act):
            with act.Fori(0, E_N // 2) as i:
                for q in range(2):
                    need(act, raw_in, 16 * (i * 2 + q) + 16)
                    need(act, y_ready, PAIR * i * TT + max(q - 1, 0) * NB * TT)
                    nc.scalar.activation(whi[:, q, :], raw[:, :], ACT.Copy).then_inc(hi_ready, 1)
                    for g in range(NB):
                        n = PAIR * i + NB * q + g
                        need(act, gu_ready, n + 1)
                        need(act, h_ready, 2 * n)
                        nc.scalar.activation(th[:, g % 2, 0, :], G[:, 0, :], ACT.Tanh, scale=0.5).then_inc(tanh_ready, 1)
                        nc.scalar.activation(th[0:F2, g % 2, 1, :], G[0:F2, 2, :], ACT.Tanh, scale=0.5).then_inc(tanh_ready, 1)
                        need(act, h_ready, 2 * n + 2)
                        need(act, y_ready, TT * (PAIR * i + NB * q + max(g - 1, 0)))
                        nc.scalar.activation(hhi[:, g % 2, 0, :], hf[:, g % 2, 0, :], ACT.Copy).then_inc(hhi_ready, 1)
                        nc.scalar.activation(hhi[0:F2, g % 2, 1, :], hf[0:F2, g % 2, 1, :], ACT.Copy).then_inc(hhi_ready, 1)

        @block.vector
        def _(dve):
            nc.vector.tensor_copy(wcol[:, :, :], wts[:, :, :].rearrange("p t e -> p e t")).then_inc(dve_link, 1)
            need(dve, dve_link, 1)
            with dve.Fori(0, E_N // 2) as i:
                for q in range(2):
                    for g in range(NB):
                        n = PAIR * i + NB * q + g
                        for r, (gate, up, k) in enumerate(((G[:, 0, :], G[:, 1, :], P), (G[0:F2, 2, :], G[F2:P, 2, :], F2))):
                            need(dve, tanh_ready, 2 * n + r + 1)
                            nc.vector.scalar_tensor_tensor(out=th[0:k, g % 2, r, :], in0=th[0:k, g % 2, r, :], scalar=1.0,
                                                           in1=gate, op0=ALU.add, op1=ALU.mult).then_inc(dve_link, 1)
                            need(dve, dve_link, 2 * n + r + 2)
                            need(dve, hlo_ready, 2 * (PAIR * i + NB * q + max(g - 1, 0)))
                            nc.vector.scalar_tensor_tensor(out=hf[0:k, g % 2, r, :], in0=th[0:k, g % 2, r, :], scalar=0.5,
                                                           in1=up, op0=ALU.mult, op1=ALU.mult).then_inc(h_ready, 1)
                        for t in range(TT):
                            need(dve, y_ready, TT * n + t + 1)
                            need(dve, added, TT * n)
                            x = X[:, g * TT + t, :]
                            nc.vector.scalar_tensor_tensor(out=x, in0=Y[:, t, :],
                                                           scalar=wcol[:, bass.ds(i * 2 + q, 1), g * TT + t],
                                                           in1=x, op0=ALU.mult, op1=ALU.add).then_inc(added, 1)

        @block.tensor
        def _(pe):
            with pe.Fori(0, E_N // 2) as i:
                for q in range(2):
                    e = i * 2 + q
                    need(pe, hi_ready, e + 1)
                    need(pe, lo_ready, e + 1)
                    for g in range(NB):
                        n = PAIR * i + NB * q + g
                        need(pe, h_ready, 2 * n)
                        for m in range(3):
                            steps = [(c, x, w) for c in range(DC) for x, w in ((xThi, whi), (xTlo, whi), (xThi, wlo))]
                            for k, (c, x, w) in enumerate(steps):
                                col = c * GUC + m * P
                                last = nc.tensor.matmul(G[:, m, :], w[:, q, col:col + P], x[:, c, g * S:(g + 1) * S],
                                                        start=(k == 0), stop=(k == len(steps) - 1))
                        last.then_inc(gu_ready, 1)
                        need(pe, hlo_ready, 2 * n + 2)
                        need(pe, added, TT * n)
                        for t in range(TT):
                            steps = [(r, h, w) for r in range(2) for h, w in ((hhi, whi), (hhi, wlo), (hlo, whi))]
                            for k, (r, h, w) in enumerate(steps):
                                kk = (P, F2)[r]
                                last = nc.tensor.matmul(Y[:, t, :], h[0:kk, g % 2, r, t * P:(t + 1) * P],
                                                        w[0:kk, q, EW + r * D:EW + (r + 1) * D],
                                                        start=(k == 0), stop=(k == len(steps) - 1))
                            last.then_inc(y_ready, 1)




def build(nc, d, out, stage=None):
    s = {
        "W": nc.dram_tensor("w_halves", [CH, P, 2 * WCH], F32).ap(),
        "BC": nc.dram_tensor("bc_rows", [NB, 2 * NST, S], F32).ap(),
        "U": nc.dram_tensor("u_store", [NB, P, DC, S], F32).ap(),
        "DT": nc.dram_tensor("dt_store", [NB, P, DC, S], F32).ap(),
        "DU": nc.dram_tensor("du_store", [NB, P, DC, S], F32).ap(),
        "X1": nc.dram_tensor("x1_store", [NB, S, D], F32).ap(),
        "X3": nc.dram_tensor("x3_store", [NB, S, D], F32).ap(),
    }
    prepare_block(nc, d, s)
    quant_block(nc, d, s)
    mix_block(nc, d, s)
    with ExitStack() as ctx:
        X = ctx.enter_context(nc.sbuf_tensor("X", [P, TILES, D], F32))
        xThi = ctx.enter_context(nc.sbuf_tensor("xThi", [P, DC, NB * S], F32R))
        xTlo = ctx.enter_context(nc.sbuf_tensor("xTlo", [P, DC, NB * S], F32R))
        wts = ctx.enter_context(nc.sbuf_tensor("wts", [P, TILES, E_N], F32))
        route_block(nc, d, s, X, xThi, xTlo, wts)
        expert_block(nc, d, out, X, xThi, xTlo, wts)


def lay_out(inputs):
    import numpy as np

    g = {k: np.asarray(v) for k, v in inputs.items()}
    idx = np.zeros((CH, P, WCH), np.int32)
    for j in range(CH):
        n = min(P, INTER - j * P)
        rows = slice(j * P, j * P + n)
        for q, name in enumerate(("L0_ffn_gate_idx", "L0_ffn_up_idx")):
            part = g[name][rows].T.reshape(DC, P, n).transpose(1, 0, 2)
            idx[j, :, q * D:(q + 1) * D].reshape(P, DC, P)[:, :, :n] = part
        idx[j, :n, 2 * D:] = g["L0_ffn_down_idx"][:, rows].T
    ew = np.zeros((E_N, P, EW + 2 * D), np.float32)
    gu = ew[:, :, :EW].reshape(E_N, P, DC, GUC)
    gate, up = (g[k].reshape(E_N, DC, P, F).transpose(0, 2, 1, 3) for k in ("L1_ffn_w_gate", "L1_ffn_w_up"))
    gu[..., :P], gu[..., P:2 * P] = gate[..., :P], up[..., :P]
    gu[..., 2 * P:2 * P + F2], gu[..., 2 * P + F2:] = gate[..., P:], up[..., P:]
    ew[:, :, EW:EW + D] = g["L1_ffn_w_down"][:, :P]
    ew[:, :F2, EW + D:] = g["L1_ffn_w_down"][:, P:]
    c = np.ascontiguousarray
    return {
        "x": g["x"], "fw": g["fside_BxS2xS2_0"], "ctx": g["ctx_1024"],
        "ctxT": c(g["ctx_1024"].transpose(0, 2, 1)), "lut": g["L0_ffn_lut"], "idx": idx,
        "inT": c(g["L1_xattn_in_proj_w"].T), "xpT": c(g["L1_xattn_x_proj_w"].T), "dpT": c(g["L1_xattn_dt_proj_w"].T),
        "convw": c(g["L1_xattn_conv_w"][:, 0, :]), "convb": c(g["L1_xattn_conv_b"].reshape(DC, P).T),
        "dtb": c(g["L1_xattn_dt_proj_b"].reshape(DC, P).T),
        "alog": c(g["L1_xattn_A_log"].reshape(DC, P, NST).transpose(1, 0, 2)),
        "dskip": c(g["L1_xattn_D"].reshape(DC, P).T),
        "gw": g["L1_ffn_gate_w"], "ew": ew,
    }


def kernel(**inputs):
    import numpy as np
    import concourse.bacc as bacc
    from concourse.bass_utils import run_bass_kernel_spmd as run

    nc = bacc.Bacc("TRN2", target_bir_lowering=False, num_devices=1)
    arrays, d = {}, {}
    for name, a in lay_out(inputs).items():
        arrays[f"in_{name}"] = a
        d[name] = nc.dram_tensor(f"in_{name}", a.shape, mybir.dt.from_np(a.dtype), kind="ExternalInput").ap()
    out = nc.dram_tensor("out_x", [NB, S, D], F32, kind="ExternalOutput").ap()
    build(nc, d, out)
    r = run(nc, [arrays], core_ids=[0])
    return r.results[0]["out_x"]
```

```python
from contextlib import ExitStack

import concourse.bass as bass
from concourse import mybir

P = 128
F32 = mybir.dt.float32
F32R = mybir.dt.float32r
BF16 = mybir.dt.bfloat16
I32 = mybir.dt.int32
U32 = mybir.dt.uint32
ALU = mybir.AluOpType
ACT = mybir.ActivationFunctionType
AX_X = mybir.AxisListType.X

NB, S, D = 4, 512, 512
DC = D // P
TT = S // P
DM = 256
MC = DM // P
NST = 16
RANK = 16
XD = RANK + 2 * NST
INTER = 1376
CH = -(-INTER // P)
LAST = INTER - (CH - 1) * P
WCH = 2 * D + D
EPS = 1e-5


class Link:

    def __init__(self, eng, sem, base=0):
        self.eng, self.sem, self.base, self.n = eng, sem, base, 0

    def __call__(self, ins):
        ins.then_inc(self.sem, 1)
        self.n += 1
        self.eng.wait_ge(self.sem, self.base + self.n)


START = 4


def need(eng, sem, n, more=0):
    eng.wait_ge(sem, n + (more + START))


def start_up(nc, sems):
    with nc.Block() as block:
        @block.sync
        def _(sp):
            for x in sems:
                sp.sem_inc(x, START)


def prepare_block(nc, d, s):
    with ExitStack() as ctx:
        sems = []

        def sb(name, shape, dt):
            return ctx.enter_context(nc.sbuf_tensor("look_" + name, shape, dt))

        def sem(name):
            sems.append(ctx.enter_context(nc.semaphore("look_" + name)))
            return sems[-1]

        idx = sb("idx", [P, WCH], I32)
        bit0 = sb("bit0", [P, WCH], I32)
        bits = [sb(f"bit{k}", [P, WCH], I32) for k in (1, 2, 3)]
        fence = sb("fence", [P, 1], F32)
        leaf = [sb(f"leaf{j}", [P, WCH], U32) for j in range(8)]
        lut = sb("lut", [P, 16], F32)
        lutx = sb("lutx", [P, 8], U32)
        whi = sb("whi", [P, WCH], F32R)
        wlo = sb("wlo", [P, WCH], F32R)

        ctxT = sb("ctxT", [P, MC, S], F32)
        inT = sb("inT", [P, MC, D], F32)
        xpT = sb("xpT", [P, DC, XD], F32)
        dpT = sb("dpT", [RANK, D], F32)
        convw = sb("convw", [P, DC, 4], F32)
        convb = sb("convb", [P, DC], F32)
        dtb = sb("dtb", [P, DC], F32)
        one = sb("one_col", [P, 1], F32)
        minus_one = sb("minus_one_col", [P, 1], F32)
        taps = sb("taps", [P, 4, S], F32)
        u = sb("u_all", [P, DC, S], F32)
        xd = sb("xd", [XD, S], F32)
        v = sb("v_all", [P, DC, S], F32)
        e = sb("e_all", [P, DC, S], F32)
        ln = sb("ln_all", [P, DC, S], F32)
        w1 = sb("w1_all", [P, DC, S], F32)
        psX = ctx.enter_context(nc.psum_tensor("look_psX", [P, DC, S], F32))
        psV = ctx.enter_context(nc.psum_tensor("look_psV", [P, DC, S], F32))

        consts_in = sem("consts_in")
        lut_in = sem("lut_in")
        idx_in = sem("idx_in")
        masks_made = sem("masks_made")
        lutx_made = sem("lutx_made")
        chosen = sem("chosen")
        split_made = sem("split_made")
        w_out = sem("w_out")
        ctx_in = ctx.enter_context(nc.semaphore("look_ctx_in"))
        proj_out = ctx.enter_context(nc.semaphore("look_proj_out"))
        stored = sem("stored")
        one_made = sem("one_made")
        x_ready = sem("x_ready")
        taps_ready = sem("taps_ready")
        conv_made = sem("conv_made")
        pool_link = sem("pool_link")
        act_link = sem("act_link")
        u_ready = sem("u_ready")
        xd_ready = sem("xd_ready")
        xd_copied = sem("xd_copied")
        dt_ready = sem("dt_ready")
        v_ready = sem("v_ready")
        one_added = sem("one_added")
        e_ready = sem("e_ready")
        ln_ready = sem("ln_ready")
        relu_ready = sem("relu_ready")
        delta_ready = sem("delta_ready")
        du_ready = sem("du_ready")
        bc_out = sem("bc_out")

        start_up(nc, sems)
        block = ctx.enter_context(nc.Block())

        @block.sync
        def _(sp):
            sp.dma_start(lut[:, :], d["lut"].rearrange("(a n) -> a n", a=1).to_broadcast([P, 16])).then_inc(lut_in, 16)
            sp.dma_start(idx[:, :], d["idx"][0]).then_inc(idx_in, 16)
            with sp.Fori(0, CH - 1) as i:
                need(sp, masks_made, 4 * i + 4)
                sp.dma_start(idx[:, :], d["idx"][i + 1]).then_inc(idx_in, 16)
                need(sp, split_made, 2 * i + 2)
                sp.dma_start(s["W"][i][:, 0:WCH], whi[:, :].bitcast(F32)).then_inc(w_out, 16)
                sp.dma_start(s["W"][i][:, WCH:2 * WCH], wlo[:, :].bitcast(F32)).then_inc(w_out, 16)
            need(sp, split_made, 2 * CH)
            sp.dma_start(s["W"][CH - 1][:, 0:WCH], whi[:, :].bitcast(F32)).then_inc(w_out, 16)
            sp.dma_start(s["W"][CH - 1][:, WCH:2 * WCH], wlo[:, :].bitcast(F32)).then_inc(w_out, 16)
            need(sp, w_out, 32 * CH)

        @block.vector
        def _(dve):
            need(dve, lut_in, 16)
            lb = lut[:, :].bitcast(U32).rearrange("p (j k) -> p j k", k=2)
            nc.vector.tensor_tensor(lutx[:, :], lb[:, :, 0], lb[:, :, 1], ALU.bitwise_xor).then_inc(lutx_made, 1)
            CHOICES = 8 + 4 + 2 + 1
            with dve.Fori(0, CH) as i:
                need(dve, lutx_made, 1)
                need(dve, idx_in, 16 * i + 16)
                nc.vector.tensor_scalar(bit0[:, :], idx[:, :], 31, 31, ALU.logical_shift_left,
                                        ALU.arith_shift_right).then_inc(masks_made, 1)
                for k in range(3):
                    nc.vector.tensor_scalar(bits[k][:, :], idx[:, :], 2 << k, None,
                                            ALU.bitwise_and).then_inc(masks_made, 1)
                need(dve, masks_made, 4 * i + 4)
                for j in range(8):
                    nc.vector.tensor_scalar(leaf[j][:, :], bit0[:, :].bitcast(U32), lutx[:, j:j + 1],
                                            lb[:, j, 0:1], ALU.bitwise_and, ALU.bitwise_xor).then_inc(chosen, 1)
                below = 8
                for k, step in enumerate((1, 2, 4)):
                    need(dve, chosen, CHOICES * i + below)
                    nc.vector.memset(fence[:, :], 0.0)
                    for j in range(0, 8, 2 * step):
                        nc.vector.copy_predicated(leaf[j][:, :], bits[k][:, :], leaf[j + step][:, :]).then_inc(chosen, 1)
                        below += 1
                need(dve, chosen, CHOICES * i + CHOICES)
                need(dve, w_out, 32 * i)
                nc.vector.tensor_copy(whi[:, :], leaf[0][:, :].bitcast(F32)).then_inc(split_made, 1)
                need(dve, split_made, 2 * i + 1)
                nc.vector.tensor_tensor(wlo[:, :], leaf[0][:, :].bitcast(F32), whi[:, :].bitcast(F32),
                                        ALU.subtract).then_inc(split_made, 1)
                need(dve, split_made, 2 * i + 2)

        @block.tensor
        def _(pe):
            need(pe, consts_in, 16 * 6)
            with pe.Fori(0, NB) as b:
                pe.wait_ge(ctx_in, 16 * b + 16)
                need(pe, taps_ready, 4 * b)
                for m in range(DC):
                    for k in range(MC):
                        last = nc.tensor.matmul(psX[:, m, :], inT[:, k, m * P:(m + 1) * P], ctxT[:, k, :],
                                                start=(k == 0), stop=(k == MC - 1))
                    last.then_inc(x_ready, 1)
                need(pe, u_ready, b + 1)
                for k in range(DC):
                    last = nc.tensor.matmul(psV[0:XD, 0, :], xpT[:, k, :], u[:, k, :], start=(k == 0), stop=(k == DC - 1))
                last.then_inc(xd_ready, 1)
                need(pe, xd_copied, b + 1)
                for m in range(DC):
                    nc.tensor.matmul(psV[:, m, :], dpT[:, m * P:(m + 1) * P], xd[0:RANK, :],
                                     start=True, stop=True).then_inc(dt_ready, 1)

        @block.scalar
        def _(act):
            act.dma_start(inT[:, :, :], d["inT"].rearrange("(k p) n -> p k n", p=P)).then_inc(consts_in, 16)
            act.dma_start(xpT[:, :, :], d["xpT"].rearrange("(k p) n -> p k n", p=P)).then_inc(consts_in, 16)
            act.dma_start(dpT[:, :], d["dpT"]).then_inc(consts_in, 16)
            act.dma_start(convw[:, :, :], d["convw"].rearrange("(c p) k -> p c k", p=P)).then_inc(consts_in, 16)
            act.dma_start(convb[:, :], d["convb"]).then_inc(consts_in, 16)
            act.dma_start(dtb[:, :], d["dtb"]).then_inc(consts_in, 16)
            need(act, consts_in, 16 * 6)
            need(act, one_made, 5)
            with act.Fori(0, NB) as b:
                for m in range(DC):
                    need(act, x_ready, DC * b + m + 1)
                    need(act, conv_made, DC * b + m)
                    for k in range(4):
                        late = 3 - k
                        if k == 3:
                            last = nc.scalar.activation(taps[:, k, :], psX[:, m, :], ACT.Identity,
                                                        bias=convb[:, m:m + 1], scale=convw[:, m, k:k + 1])
                        else:
                            last = nc.scalar.activation(taps[:, k, late:S], psX[:, m, 0:S - late], ACT.Copy,
                                                        scale=convw[:, m, k:k + 1])
                    last.then_inc(taps_ready, 1)
                need(act, conv_made, DC * b + DC)
                need(act, stored, b)
                nc.scalar.activation(u[:, :, :], v[:, :, :], ACT.Silu).then_inc(u_ready, 1)
                need(act, xd_ready, b + 1)
                need(act, bc_out, 16 * b)
                nc.scalar.activation(xd[:, :], psV[0:XD, 0, :], ACT.Copy).then_inc(xd_copied, 1)
                need(act, u_ready, b + 1)
                for m in range(DC):
                    need(act, dt_ready, DC * b + m + 1)
                    nc.scalar.activation(v[:, m, :], psV[:, m, :], ACT.Identity, bias=dtb[:, m:m + 1]).then_inc(v_ready, 1)
                need(act, v_ready, DC * b + DC)
                nc.scalar.activation(w1[:, :, :], v[:, :, :], ACT.Abs).then_inc(act_link, 1)
                need(act, act_link, b + 1)
                nc.scalar.activation(e[:, :, :], w1[:, :, :], ACT.Exp, scale=-1.0).then_inc(e_ready, 1)
                need(act, e_ready, b + 1)
                nc.scalar.activation(w1[:, :, :], e[:, :, :], ACT.Identity, bias=one[:, :]).then_inc(one_added, 1)
                need(act, one_added, 2 * b + 1)
                nc.scalar.activation(w1[:, :, :], w1[:, :, :], ACT.Identity, bias=minus_one[:, :]).then_inc(one_added, 1)
                nc.scalar.activation(ln[:, :, :], e[:, :, :], ACT.Ln, bias=one[:, :]).then_inc(ln_ready, 1)
                nc.scalar.activation(v[:, :, :], v[:, :, :], ACT.Relu).then_inc(relu_ready, 1)
                need(act, xd_copied, b + 1)
                act.dma_start(s["BC"][b], xd[RANK:XD, :]).then_inc(bc_out, 16)
            need(act, bc_out, 16 * NB)

        @block.gpsimd
        def _(pool):
            nc.gpsimd.memset(one[:, :], 1.0).then_inc(one_made, 1)
            nc.gpsimd.memset(minus_one[:, :], -1.0).then_inc(one_made, 1)
            for k in range(3):
                nc.gpsimd.memset(taps[:, k, 0:3 - k], 0.0).then_inc(one_made, 1)
            PER = 2 * DC + 2
            with pool.Fori(0, NB) as b:
                link = Link(pool, pool_link, b * PER + START)
                need(pool, x_ready, DC * b)
                pool.dma_start(ctxT[:, :, :], d["ctxT"][b].rearrange("(k p) n -> p k n", p=P)).then_inc(ctx_in, 16)
                need(pool, delta_ready, b)
                for m in range(DC):
                    need(pool, taps_ready, DC * b + m + 1)
                    link(nc.gpsimd.tensor_tensor(taps[:, 3, :], taps[:, 3, :], taps[:, 2, :], ALU.add))
                    link(nc.gpsimd.tensor_tensor(taps[:, 3, :], taps[:, 3, :], taps[:, 1, :], ALU.add))
                    nc.gpsimd.tensor_tensor(v[:, m, :], taps[:, 3, :], taps[:, 0, :], ALU.add).then_inc(conv_made, 1)
                need(pool, one_added, 2 * b + 2)
                link(nc.gpsimd.tensor_tensor(w1[:, :, :], e[:, :, :], w1[:, :, :], ALU.subtract))
                need(pool, ln_ready, b + 1)
                link(nc.gpsimd.tensor_tensor(w1[:, :, :], ln[:, :, :], w1[:, :, :], ALU.add))
                need(pool, relu_ready, b + 1)
                nc.gpsimd.tensor_tensor(v[:, :, :], v[:, :, :], w1[:, :, :], ALU.add).then_inc(delta_ready, 1)
                need(pool, delta_ready, b + 1)
                nc.gpsimd.tensor_tensor(w1[:, :, :], v[:, :, :], u[:, :, :], ALU.mult).then_inc(du_ready, 1)
                need(pool, du_ready, b + 1)
                pool.dma_start(s["U"][b], u[:, :, :]).then_inc(proj_out, 16)
                pool.dma_start(s["DT"][b], v[:, :, :]).then_inc(proj_out, 16)
                pool.dma_start(s["DU"][b], w1[:, :, :]).then_inc(proj_out, 16)
                pool.wait_ge(proj_out, 48 * b + 48)
                pool.sem_inc(stored, 1)


MAGIC = 1.5 * 2.0 ** 23
QMAX = 127.0
QEPS = 1e-6
GU = 256


def quant_block(nc, d, s):
    with ExitStack() as ctx:
        def sb(name, shape, dt):
            return ctx.enter_context(nc.sbuf_tensor("quant_" + name, shape, dt))

        def sem(name):
            return ctx.enter_context(nc.semaphore("quant_" + name))

        ident = sb("ident", [P, P], F32)
        identb = sb("identb", [P, P], BF16)
        ones = sb("ones", [P, P], F32)
        eps = sb("eps_col", [P, 1], F32)
        magic = sb("magic_col", [P, 1], F32)
        xt = sb("xt", [P, TT, D], F32)
        wt = sb("wt", [P, TT, D], F32)
        ct = sb("ct", [P, TT, GU], F32)
        xn = sb("xn", [P, TT, D], F32)
        a = sb("a", [P, TT, GU], F32)
        sg = sb("sg", [P, TT, GU], F32)
        h = sb("h", [P, TT, D], F32)
        xs = sb("xs", [P, TT, D], F32)
        ws = sb("ws", [P, TT, D], F32)
        xq = sb("xq", [P, TT, D], BF16)
        wq = sb("wq", [P, TT, D], BF16)
        xqT = sb("xqT", [P, DC, S], BF16)
        wqT = sb("wqT", [P, DC, S], BF16)
        dg = sb("dg", [P, 3, DC, P], F32)
        wscB = sb("wscB", [P, S], F32)
        xo = sb("xo", [P, TT, D], F32)
        stats = sb("stats", [P, TT, 6], F32)
        mv = sb("mv", [P, TT, 2], F32)
        rstd = sb("rstd", [P, TT], F32)
        nmr = sb("nmr", [P, TT], F32)
        ax = sb("ax", [P, DC], F32)
        aw = sb("aw", [P, DC], F32)
        sc = sb("sc", [P, 2, DC], F32)
        xm = sb("xm", [P, 2, TT], F32)
        xsc = sb("xsc", [P, 2, TT], F32)
        inv = sb("inv", [P, 2, TT], F32)
        T = ctx.enter_context(nc.psum_tensor("quant_T", [P, 4, S], F32))
        U = ctx.enter_context(nc.psum_tensor("quant_U", [P, 4, S], F32))

        pool_made = sem("pool_made")
        x_in = sem("x_in")
        w_in = sem("w_in")
        c_in = sem("c_in")
        dve_link = sem("dve_link")
        var_ready = sem("var_ready")
        std_ready = sem("std_ready")
        rstd_ready = sem("rstd_ready")
        xn_ready = sem("xn_ready")
        xT_ready = sem("xT_ready")
        wT_ready = sem("wT_ready")
        ax_ready = sem("ax_ready")
        ratio_ready = sem("ratio_ready")
        s_ready = sem("s_ready")
        diag_ready = sem("diag_ready")
        rows_ready = sem("rows_ready")
        ws_ready = sem("ws_ready")
        wdiag_ready = sem("wdiag_ready")
        wrow_ready = sem("wrow_ready")
        wrow_copied = sem("wrow_copied")
        shifted = sem("shifted")
        xq_ready = sem("xq_ready")
        wq_ready = sem("wq_ready")
        xqT_ready = sem("xqT_ready")
        wqT_ready = sem("wqT_ready")
        xqT_copied = sem("xqT_copied")
        wqT_copied = sem("wqT_copied")
        out_ready = sem("out_ready")
        h_ready = sem("h_ready")
        silu_ready = sem("silu_ready")
        a_ready = sem("a_ready")
        x1_ready = sem("x1_ready")
        x1_out = sem("x1_out")

        block = ctx.enter_context(nc.Block())

        @block.gpsimd
        def _(pool):
            nc.gpsimd.memset(ident[:, :], 0.0).then_inc(pool_made, 1)
            nc.gpsimd.memset(identb[:, :], 0.0).then_inc(pool_made, 1)
            nc.gpsimd.memset(ones[:, :], 1.0).then_inc(pool_made, 1)
            nc.gpsimd.memset(eps[:, :], EPS).then_inc(pool_made, 1)
            nc.gpsimd.memset(magic[:, :], MAGIC).then_inc(pool_made, 1)
            pool.wait_ge(pool_made, 5)
            for m in (ident, identb):
                nc.gpsimd.affine_select(out=m[:, :], in_=m[:, :], compare_op=ALU.not_equal, fill=1.0, base=0,
                                        pattern=[[-1, P]], channel_multiplier=1).then_inc(pool_made, 1)

        @block.sync
        def _(sp):
            sp.dma_start(xt[:, :, :], d["x"][0].rearrange("(t p) n -> p t n", p=P)).then_inc(x_in, 16)
            sp.dma_start(wt[:, :, :], d["fw"][0].rearrange("(t p) n -> p t n", p=P)).then_inc(w_in, 16)
            sp.dma_start(ct[:, :, :], d["ctx"][0].rearrange("(t p) n -> p t n", p=P)).then_inc(c_in, 16)
            for b in range(NB):
                if b + 1 < NB:
                    sp.wait_ge(ws_ready, 2 * b + 1)
                    sp.dma_start(wt[:, :, :], d["fw"][b + 1].rearrange("(t p) n -> p t n", p=P)).then_inc(w_in, 16)
                    sp.wait_ge(ws_ready, 2 * b + 2)
                    sp.dma_start(ct[:, :, :], d["ctx"][b + 1].rearrange("(t p) n -> p t n", p=P)).then_inc(c_in, 16)
                sp.wait_ge(x1_ready, b + 1)
                if b + 1 < NB:
                    sp.dma_start(xt[:, :, :], d["x"][b + 1].rearrange("(t p) n -> p t n", p=P)).then_inc(x_in, 16)
                sp.dma_start(s["X1"][b].rearrange("(t p) n -> p t n", p=P), xo[:, :, :]).then_inc(x1_out, 16)
            sp.wait_ge(x1_out, 16 * NB)

        def linears():
            for b in range(NB):
                for lin in range(2):
                    n = 2 * b + lin
                    x, w, nd = ((xn, wt, DC), (a, ct, GU // P))[lin]
                    yield b, lin, n, x, w, nd

        @block.tensor
        def _(pe):
            pe.wait_ge(pool_made, 7)
            for b, lin, n, x, w, nd in linears():
                if lin == 0:
                    pe.wait_ge(xn_ready, TT * b + TT)
                    pe.wait_ge(w_in, 16 * b + 16)
                else:
                    pe.wait_ge(a_ready, b + 1)
                    pe.wait_ge(c_in, 16 * b + 16)
                if n > 0:
                    pe.wait_ge(h_ready, TT * n)
                for c in range(nd):
                    for t in range(TT):
                        last = nc.tensor.transpose(T[:, c, t * P:(t + 1) * P], x[:, t, c * P:(c + 1) * P], ident[:, :])
                last.then_inc(xT_ready, 1)
                for c in range(nd):
                    for t in range(TT):
                        last = nc.tensor.transpose(U[:, c, t * P:(t + 1) * P], w[:, t, c * P:(c + 1) * P], ident[:, :])
                last.then_inc(wT_ready, 1)
                pe.wait_ge(diag_ready, 2 * n + 2)
                for q in range(2):
                    for c in range(nd):
                        last = nc.tensor.matmul(T[:, q, c * P:(c + 1) * P], ones[:, :], dg[:, q, c, :],
                                                start=True, stop=True)
                last.then_inc(rows_ready, 1)
                pe.wait_ge(wdiag_ready, n + 1)
                for c in range(TT):
                    last = nc.tensor.matmul(T[:, 2, c * P:(c + 1) * P], ones[:, :], dg[:, 2, c, :], start=True, stop=True)
                last.then_inc(wrow_ready, 1)
                pe.wait_ge(wrow_copied, n + 1)
                pe.wait_ge(xq_ready, n + 1)
                for c in range(nd):
                    for t in range(TT):
                        last = nc.tensor.transpose(T[:, c, 0:S // 2].bitcast(BF16)[:, t * P:(t + 1) * P],
                                                   xq[:, t, c * P:(c + 1) * P], identb[:, :])
                last.then_inc(xqT_ready, 1)
                pe.wait_ge(wq_ready, n + 1)
                for c in range(nd):
                    for t in range(TT):
                        last = nc.tensor.transpose(U[:, c, 0:S // 2].bitcast(BF16)[:, t * P:(t + 1) * P],
                                                   wq[:, t, c * P:(c + 1) * P], identb[:, :])
                last.then_inc(wqT_ready, 1)
                pe.wait_ge(xqT_copied, n + 1)
                pe.wait_ge(wqT_copied, n + 1)
                for t in range(TT):
                    for c in range(nd):
                        last = nc.tensor.matmul(U[:, t, :], xqT[:, c, t * P:(t + 1) * P], wqT[:, c, :],
                                                start=(c == 0), stop=(c == nd - 1))
                    last.then_inc(out_ready, 1)

        @block.scalar
        def _(act):
            act.wait_ge(pool_made, 7)
            for b, lin, n, x, w, nd in linears():
                if lin == 0:
                    act.wait_ge(var_ready, TT * b + TT)
                    nc.scalar.activation(rstd[:, :], mv[:, :, 1], ACT.Sqrt, bias=eps[:, :]).then_inc(std_ready, 1)
                    act.wait_ge(rstd_ready, b + 1)
                    for t in range(TT):
                        nc.scalar.activation(xn[:, t, :], xt[:, t, :], ACT.Identity, bias=nmr[:, t:t + 1],
                                             scale=rstd[:, t:t + 1]).then_inc(xn_ready, 1)
                act.wait_ge(ratio_ready, n + 1)
                nc.scalar.activation(sc[:, 1, 0:nd], sc[:, 0, 0:nd], ACT.Sqrt).then_inc(s_ready, 1)
                act.wait_ge(wrow_ready, n + 1)
                nc.scalar.activation(wscB[:, :], T[:, 2, :], ACT.Copy).then_inc(wrow_copied, 1)
                for q, r in enumerate((xs, ws)):
                    for t in range(TT):
                        nc.scalar.activation(r[:, t, 0:nd * P], r[:, t, 0:nd * P], ACT.Identity, bias=magic[:, :],
                                             scale=inv[:, q, t:t + 1]).then_inc(shifted, 1)
                act.wait_ge(xqT_ready, n + 1)
                nc.scalar.activation(xqT[:, 0:nd, :], T[:, 0:nd, 0:S // 2].bitcast(BF16), ACT.Copy).then_inc(xqT_copied, 1)
                if lin == 0:
                    act.wait_ge(h_ready, TT * n + TT)
                    nc.scalar.activation(sg[:, :, :], h[:, :, 0:GU], ACT.Silu).then_inc(silu_ready, 1)

        @block.vector
        def _(dve):
            dve.wait_ge(pool_made, 7)
            link = Link(dve, dve_link)
            for b, lin, n, x, w, nd in linears():
                W = nd * P
                if lin == 0:
                    dve.wait_ge(x_in, 16 * b + 16)
                    for t in range(TT):
                        link(nc.vector.bn_stats(stats[:, t, :], xt[:, t, :]))
                    for t in range(TT):
                        nc.vector.bn_aggr(mv[:, t, :], stats[:, t, :]).then_inc(var_ready, 1)
                    dve.wait_ge(std_ready, b + 1)
                    link(nc.vector.reciprocal(rstd[:, :], rstd[:, :]))
                    nc.vector.scalar_tensor_tensor(out=nmr[:, :], in0=mv[:, :, 0], scalar=-1.0, in1=rstd[:, :],
                                                   op0=ALU.mult, op1=ALU.mult).then_inc(rstd_ready, 1)
                for m, ps, ready in ((ax, T, xT_ready), (aw, U, wT_ready)):
                    dve.wait_ge(ready, n + 1)
                    link(nc.vector.tensor_reduce(m[:, 0:nd], ps[:, 0:nd, :], AX_X, ALU.max, apply_absolute_value=True))
                    link(nc.vector.tensor_scalar(m[:, 0:nd], m[:, 0:nd], QEPS, None, ALU.max))
                link(nc.vector.reciprocal(aw[:, 0:nd], aw[:, 0:nd]))
                nc.vector.tensor_tensor(sc[:, 0, 0:nd], ax[:, 0:nd], aw[:, 0:nd], ALU.mult).then_inc(ratio_ready, 1)
                dve.wait_ge(s_ready, n + 1)
                link(nc.vector.tensor_scalar(sc[:, 1, 0:nd], sc[:, 1, 0:nd], QEPS, None, ALU.max))
                link(nc.vector.reciprocal(sc[:, 0, 0:nd], sc[:, 1, 0:nd]))
                for q in range(2):
                    nc.vector.tensor_tensor(dg[:, q, 0:nd, :], ident[:, :].unsqueeze(1).to_broadcast([P, nd, P]),
                                            sc[:, q, 0:nd].unsqueeze(2).to_broadcast([P, nd, P]),
                                            ALU.mult).then_inc(diag_ready, 1)
                dve.wait_ge(rows_ready, n + 1)
                nc.vector.tensor_tensor(ws[:, :, 0:W], w[:, :, 0:W], T[:, 1, 0:W].unsqueeze(1).to_broadcast([P, TT, W]),
                                        ALU.mult).then_inc(ws_ready, 1)
                link(nc.vector.tensor_tensor(xs[:, :, 0:W], x[:, :, 0:W],
                                             T[:, 0, 0:W].unsqueeze(1).to_broadcast([P, TT, W]), ALU.mult))
                dve.wait_ge(ws_ready, n + 1)
                link(nc.vector.tensor_reduce(xm[:, 1, :], ws[:, :, 0:W], AX_X, ALU.max, apply_absolute_value=True))
                link(nc.vector.tensor_reduce(xm[:, 0, :], xs[:, :, 0:W], AX_X, ALU.max, apply_absolute_value=True))
                link(nc.vector.tensor_scalar(xsc[:, :, :], xm[:, :, :], QEPS, 1.0 / QMAX, ALU.max, ALU.mult))
                link(nc.vector.reciprocal(inv[:, :, :], xsc[:, :, :]))
                nc.vector.tensor_tensor(dg[:, 2, :, :], ident[:, :].unsqueeze(1).to_broadcast([P, TT, P]),
                                        xsc[:, 1, :].unsqueeze(2).to_broadcast([P, TT, P]), ALU.mult).then_inc(wdiag_ready, 1)
                for q, (r, o, ready) in enumerate(((xs, xq, xq_ready), (ws, wq, wq_ready))):
                    dve.wait_ge(shifted, 2 * TT * n + TT * (q + 1))
                    link(nc.vector.tensor_scalar(o[:, :, 0:W], r[:, :, 0:W], MAGIC, QMAX, ALU.subtract, ALU.min))
                    nc.vector.tensor_scalar(o[:, :, 0:W], o[:, :, 0:W], -QMAX, None, ALU.max).then_inc(ready, 1)
                dve.wait_ge(wqT_ready, n + 1)
                nc.vector.tensor_copy(wqT[:, 0:nd, :], U[:, 0:nd, 0:S // 2].bitcast(BF16)).then_inc(wqT_copied, 1)
                for t in range(TT):
                    dve.wait_ge(out_ready, TT * n + t + 1)
                    dve.wait_ge(wrow_copied, n + 1)
                    nc.vector.scalar_tensor_tensor(out=h[:, t, :], in0=U[:, t, :], scalar=xsc[:, 0, t:t + 1],
                                                   in1=wscB[:, :], op0=ALU.mult, op1=ALU.mult).then_inc(h_ready, 1)
                dve.wait_ge(h_ready, TT * n + TT)
                if lin == 0:
                    dve.wait_ge(silu_ready, b + 1)
                    nc.vector.tensor_tensor(a[:, :, :], sg[:, :, :], h[:, :, GU:2 * GU], ALU.mult).then_inc(a_ready, 1)
                    dve.wait_ge(a_ready, b + 1)
                else:
                    if b > 0:
                        dve.wait_ge(x1_out, 16 * b)
                    nc.vector.tensor_tensor(xo[:, :, :], xt[:, :, :], h[:, :, :], ALU.add).then_inc(x1_ready, 1)


NG = 4
UNITS = (NST // NG) * DC
WBUF = 3


def mix_block(nc, d, s):
    with ExitStack() as ctx:
        sems = []

        def sb(name, shape, dt):
            return ctx.enter_context(nc.sbuf_tensor("mix_" + name, shape, dt))

        def sem(name):
            sems.append(ctx.enter_context(nc.semaphore("mix_" + name)))
            return sems[-1]

        ident = sb("ident", [P, P], F32)
        eps = sb("eps_col", [P, 1], F32)
        fence = sb("fence", [P, 1], F32)
        A = sb("A", [P, DC, NST], F32)
        dskip = sb("dskip", [P, DC], F32)
        xt = sb("xt", [P, TT, D], F32)
        xn = sb("xn", [P, TT, D], F32)
        xo = sb("xo", [P, TT, D], F32)
        xThi = sb("xThi", [P, DC, S], F32R)
        xTlo = sb("xTlo", [P, DC, S], F32R)
        stats = sb("stats", [P, TT, 6], F32)
        mv = sb("mv", [P, TT, 2], F32)
        rstd = sb("rstd", [P, TT], F32)
        nmr = sb("nmr", [P, TT], F32)
        w = sb("w", [P, WBUF, 2 * WCH], F32R)
        th = sb("th", [P, 2, S], F32)
        hf = sb("hf", [P, 2, S], F32)
        hhi = sb("hhi", [P, 2, S], F32R)
        hlo = sb("hlo", [P, 2, S], F32R)
        dt = sb("dt", [P, DC, S], F32)
        du = sb("du", [P, DC, S], F32)
        u = sb("u", [P, DC, S], F32)
        y = sb("y", [P, DC, S], F32)
        Bb = sb("Bb", [P, 2, NG, S], F32)
        Cb = sb("Cb", [P, 2, NG, S], F32)
        dA = sb("dA", [P, 2, NG, S], F32)
        st = sb("st", [P, 2, NG, S], F32)
        G = ctx.enter_context(nc.psum_tensor("mix_G", [P, 2, 2, S], F32))
        Dp = ctx.enter_context(nc.psum_tensor("mix_Dp", [P, TT, S], F32))

        const_in = sem("const_in")
        pool_made = sem("pool_made")
        x_in = sem("x_in")
        proj_in = sem("proj_in")
        w_in = [sem(f"w_in{i}") for i in range(WBUF)]
        bc_in = [sem(f"bc_in{i}") for i in range(2)]
        a_made = sem("a_made")
        dve_link = sem("dve_link")
        var_ready = sem("var_ready")
        std_ready = sem("std_ready")
        rstd_ready = sem("rstd_ready")
        xn_ready = sem("xn_ready")
        xT_ready = sem("xT_ready")
        hi_ready = sem("hi_ready")
        lo_ready = sem("lo_ready")
        gu_ready = sem("gu_ready")
        tanh_ready = sem("tanh_ready")
        h_ready = sem("h_ready")
        hhi_ready = sem("hhi_ready")
        hlo_ready = sem("hlo_ready")
        chunk_done = sem("chunk_done")
        da_ready = sem("da_ready")
        dbu_ready = sem("dbu_ready")
        unit_done = sem("unit_done")
        x2_ready = sem("x2_ready")
        z_ready = sem("z_ready")
        gated = sem("gated")
        gT_ready = sem("gT_ready")
        x3_ready = sem("x3_ready")
        x3_out = sem("x3_out")
        start_up(nc, sems)
        block = ctx.enter_context(nc.Block())

        SLOT = [j * UNITS // CH for j in range(CH)]

        @block.gpsimd
        def _(pool):
            nc.gpsimd.memset(eps[:, :], EPS).then_inc(pool_made, 1)
            nc.gpsimd.memset(ident[:, :], 0.0).then_inc(pool_made, 1)
            nc.gpsimd.memset(dA[:, :, :, 0:1], 0.0).then_inc(pool_made, 1)
            need(pool, pool_made, 3)
            nc.gpsimd.affine_select(out=ident[:, :], in_=ident[:, :], compare_op=ALU.not_equal, fill=1.0, base=0,
                                    pattern=[[-1, P]], channel_multiplier=1).then_inc(pool_made, 1)
            with pool.Fori(0, NB) as b:
                def low_half(j):
                    need(pool, hhi_ready, CH * b + j + 1)
                    need(pool, chunk_done, CH * b + max(j - 1, 0))
                    nc.gpsimd.tensor_tensor(hlo[:, j % 2, :], hf[:, j % 2, :], hhi[:, j % 2, :].bitcast(F32),
                                            ALU.subtract).then_inc(hlo_ready, 1)

                need(pool, proj_in, 48 * b + 48)
                for k in range(UNITS):
                    ng, c = divmod(k, DC)
                    if k % DC == 0:
                        need(pool, bc_in[ng % 2], 32 * (NST // NG // 2) * b + 32 * (ng // 2 + 1))
                    need(pool, unit_done, UNITS * b + max(k - 1, 0))
                    nc.gpsimd.tensor_tensor(st[:, k % 2, :, :], Bb[:, ng % 2, :, :],
                                            du[:, c, :].unsqueeze(1).to_broadcast([P, NG, S]),
                                            ALU.mult).then_inc(dbu_ready, 1)
                    for j in range(CH):
                        if SLOT[j] == k:
                            low_half(j)

        @block.sync
        def _(sp):
            sp.dma_start(A[:, :, :], d["alog"]).then_inc(const_in, 16)
            sp.dma_start(dskip[:, :], d["dskip"]).then_inc(const_in, 16)
            with sp.Fori(0, NB) as b:
                def load_w(j):
                    need(sp, chunk_done, CH * b + max(j - WBUF + 1, 0))
                    sp.dma_start(w[:, j % WBUF, :].bitcast(F32), s["W"][j]).then_inc(w_in[j % WBUF], 16)

                def load_bc(ng):
                    need(sp, unit_done, UNITS * b + max(DC * (ng - 1), 0))
                    for dst, at in ((Bb, 0), (Cb, NST)):
                        sp.dma_start(dst[:, ng % 2, :, :],
                                     s["BC"][b][at + NG * ng:at + NG * ng + NG, :].unsqueeze(0).to_broadcast([P, NG, S])
                                     ).then_inc(bc_in[ng % 2], 16)

                need(sp, x3_ready, b)
                sp.dma_start(xt[:, :, :], s["X1"][b].rearrange("(t p) n -> p t n", p=P)).then_inc(x_in, 16)
                for dst, name in ((dt, "DT"), (du, "DU"), (u, "U")):
                    sp.dma_start(dst[:, :, :], s[name][b]).then_inc(proj_in, 16)
                load_bc(0)
                for j in range(WBUF):
                    load_w(j)
                load_bc(1)
                for j in range(WBUF, CH):
                    load_w(j)
                    if j in (6, 9):
                        load_bc(2 if j == 6 else 3)
                need(sp, x3_ready, b + 1)
                sp.dma_start(s["X3"][0:NB * S, :].rearrange("(b t p) n -> b p t n", b=NB, p=P)[b], xo[:, :, :]).then_inc(x3_out, 16)
            need(sp, x3_out, 16 * NB)

        @block.tensor
        def _(pe):
            need(pe, pool_made, 4)
            with pe.Fori(0, NB) as b:
                need(pe, xn_ready, 2 * TT * b + TT)
                need(pe, x3_ready, b)
                for c in range(DC):
                    for t in range(TT):
                        last = nc.tensor.transpose(Dp[:, c, t * P:(t + 1) * P], xn[:, t, c * P:(c + 1) * P], ident[:, :])
                last.then_inc(xT_ready, 1)
                need(pe, hi_ready, b + 1)
                need(pe, lo_ready, b + 1)

                def up(j):
                    need(pe, w_in[j % WBUF], 16 * len(range(j % WBUF, CH, WBUF)) * b + 16 * (j // WBUF + 1))
                    need(pe, h_ready, CH * b + max(j - 1, 0))
                    wb = w[:, j % WBUF, :]
                    for q in range(2):
                        steps = [(c, x, at) for c in range(DC) for x, at in ((xThi, 0), (xTlo, 0), (xThi, WCH))]
                        for i, (c, x, at) in enumerate(steps):
                            col = at + q * D + c * P
                            last = nc.tensor.matmul(G[:, j % 2, q, :], wb[:, col:col + P], x[:, c, :],
                                                    start=(i == 0), stop=(i == len(steps) - 1))
                    last.then_inc(gu_ready, 1)

                def down(j):
                    need(pe, hlo_ready, CH * b + j + 1)
                    n = P if j < CH - 1 else LAST
                    wb = w[:, j % WBUF, :]
                    for t in range(TT):
                        for i, (h, at) in enumerate(((hhi, 0), (hhi, WCH), (hlo, 0))):
                            last = nc.tensor.matmul(Dp[:, t, :], h[0:n, j % 2, t * P:(t + 1) * P],
                                                    wb[0:n, at + 2 * D:at + 3 * D],
                                                    start=(j == 0 and i == 0), stop=(j == CH - 1 and i == 2))
                    last.then_inc(chunk_done, 1)

                up(0)
                for j in range(CH):
                    if j + 1 < CH:
                        up(j + 1)
                    down(j)
                need(pe, gated, b + 1)
                for t in range(TT):
                    for c in range(DC):
                        last = nc.tensor.transpose(Dp[:, t, c * P:(c + 1) * P], y[:, c, t * P:(t + 1) * P], ident[:, :])
                last.then_inc(gT_ready, 1)

        @block.scalar
        def _(act):
            need(act, const_in, 32)
            need(act, pool_made, 4)
            nc.scalar.activation(A[:, :, :], A[:, :, :], ACT.Exp).then_inc(a_made, 1)
            need(act, a_made, 1)
            nc.scalar.mul(A[:, :, :], A[:, :, :], -1.0).then_inc(a_made, 1)
            need(act, a_made, 2)

            def normalise(n):
                need(act, var_ready, n + 1)
                nc.scalar.activation(rstd[:, :], mv[:, :, 1], ACT.Sqrt, bias=eps[:, :]).then_inc(std_ready, 1)
                need(act, rstd_ready, n + 1)
                for t in range(TT):
                    nc.scalar.activation(xn[:, t, :], xt[:, t, :], ACT.Identity, bias=nmr[:, t:t + 1],
                                         scale=rstd[:, t:t + 1]).then_inc(xn_ready, 1)

            with act.Fori(0, NB) as b:
                def tanh(j):
                    need(act, gu_ready, CH * b + j + 1)
                    need(act, h_ready, CH * b + max(j - 1, 0))
                    nc.scalar.activation(th[:, j % 2, :], G[:, j % 2, 0, :], ACT.Tanh, scale=0.5).then_inc(tanh_ready, 1)

                def high_half(j):
                    need(act, h_ready, CH * b + j + 1)
                    need(act, chunk_done, CH * b + max(j - 1, 0))
                    nc.scalar.activation(hhi[:, j % 2, :], hf[:, j % 2, :], ACT.Copy).then_inc(hhi_ready, 1)

                need(act, gated, b)
                normalise(2 * b)
                need(act, xT_ready, b + 1)
                nc.scalar.activation(xThi[:, :, :], Dp[:, :, :], ACT.Copy).then_inc(hi_ready, 1)
                need(act, proj_in, 48 * b + 48)
                for k in range(UNITS):
                    ng, c = divmod(k, DC)
                    for j in range(CH):
                        if SLOT[j] == k:
                            tanh(j)
                    need(act, unit_done, UNITS * b + max(k - 1, 0))
                    for n in range(NG):
                        m = NG * ng + n
                        last = nc.scalar.activation(dA[:, k % 2, n, 1:S], dt[:, c, 1:S], ACT.Exp, scale=A[:, c, m:m + 1])
                    last.then_inc(da_ready, 1)
                    for j in range(CH):
                        if SLOT[j] == k:
                            high_half(j)
                normalise(2 * b + 1)
                need(act, xn_ready, 2 * TT * b + 2 * TT)
                nc.scalar.activation(xn[:, :, :], xn[:, :, :], ACT.Silu).then_inc(z_ready, 1)

        @block.vector
        def _(dve):
            LINKS = 2 * (TT + 1) + (UNITS - DC) * 4 + DC * 3 + CH + DC
            need(dve, pool_made, 4)
            with dve.Fori(0, NB) as b:
                link = Link(dve, dve_link, b * LINKS + START)

                def moments(n):
                    for t in range(TT):
                        link(nc.vector.bn_stats(stats[:, t, :], xt[:, t, :]))
                    nc.vector.memset(fence[:, :], 0.0)
                    for t in range(TT):
                        last = nc.vector.bn_aggr(mv[:, t, :], stats[:, t, :])
                    last.then_inc(var_ready, 1)
                    need(dve, std_ready, n + 1)
                    link(nc.vector.reciprocal(rstd[:, :], rstd[:, :]))
                    nc.vector.scalar_tensor_tensor(out=nmr[:, :], in0=mv[:, :, 0], scalar=-1.0, in1=rstd[:, :],
                                                   op0=ALU.mult, op1=ALU.mult).then_inc(rstd_ready, 1)

                def hidden(j):
                    need(dve, tanh_ready, CH * b + j + 1)
                    link(nc.vector.scalar_tensor_tensor(out=th[:, j % 2, :], in0=th[:, j % 2, :], scalar=1.0,
                                                        in1=G[:, j % 2, 0, :], op0=ALU.add, op1=ALU.mult))
                    need(dve, hlo_ready, CH * b + max(j - 1, 0))
                    nc.vector.scalar_tensor_tensor(out=hf[:, j % 2, :], in0=th[:, j % 2, :], scalar=0.5,
                                                   in1=G[:, j % 2, 1, :], op0=ALU.mult, op1=ALU.mult).then_inc(h_ready, 1)

                need(dve, x_in, 16 * b + 16)
                moments(2 * b)
                need(dve, hi_ready, b + 1)
                nc.vector.tensor_tensor(xTlo[:, :, :], Dp[:, :, :], xThi[:, :, :].bitcast(F32),
                                        ALU.subtract).then_inc(lo_ready, 1)
                for k in range(UNITS):
                    ng, c = divmod(k, DC)
                    r = st[:, k % 2, :, :]
                    for j in range(CH):
                        if SLOT[j] == k:
                            hidden(j)
                    need(dve, da_ready, UNITS * b + k + 1)
                    need(dve, dbu_ready, UNITS * b + k + 1)
                    flat = r.rearrange("p n s -> p (n s)")
                    link(nc.vector.tensor_tensor_scan(flat, dA[:, k % 2, :, :].rearrange("p n s -> p (n s)"), flat, 0.0,
                                                      ALU.mult, ALU.add))
                    need(dve, bc_in[ng % 2], 32 * (NST // NG // 2) * b + 32 * (ng // 2 + 1))
                    link(nc.vector.tensor_tensor(r, r, Cb[:, ng % 2, :, :], ALU.mult))
                    link(nc.vector.tensor_tensor(r[:, 0:2, :], r[:, 0:2, :], r[:, 2:4, :], ALU.add))
                    if ng == 0:
                        nc.vector.tensor_tensor(y[:, c, :], r[:, 0, :], r[:, 1, :], ALU.add).then_inc(unit_done, 1)
                    else:
                        link(nc.vector.tensor_tensor(r[:, 0, :], r[:, 0, :], r[:, 1, :], ALU.add))
                        nc.vector.tensor_tensor(y[:, c, :], y[:, c, :], r[:, 0, :], ALU.add).then_inc(unit_done, 1)
                need(dve, unit_done, UNITS * b + UNITS)
                need(dve, chunk_done, CH * b + CH)
                nc.vector.tensor_tensor(xt[:, :, :], xt[:, :, :], Dp[:, :, :], ALU.add).then_inc(x2_ready, 1)
                need(dve, x2_ready, b + 1)
                moments(2 * b + 1)
                for c in range(DC):
                    link(nc.vector.scalar_tensor_tensor(out=y[:, c, :], in0=u[:, c, :], scalar=dskip[:, c:c + 1],
                                                        in1=y[:, c, :], op0=ALU.mult, op1=ALU.add))
                need(dve, z_ready, b + 1)
                nc.vector.tensor_tensor(y[:, :, :], y[:, :, :], xn[:, :, :], ALU.mult).then_inc(gated, 1)
                need(dve, gT_ready, b + 1)
                need(dve, x3_out, 16 * b)
                nc.vector.tensor_tensor(xo[:, :, :], xt[:, :, :], Dp[:, :, :], ALU.add).then_inc(x3_ready, 1)
                assert link.n == LINKS, (link.n, LINKS)


E_N = 32
F = 192
F2 = F - P
TOP = 8
TILES = NB * TT
CAP = 2 * (NB * S * TOP // E_N)
GUC = 3 * P
EW = DC * GUC


SUBS = CAP // P
PAIRS = SUBS // 2
AWAY = float(4 * E_N * CAP)
ROWS = NB * S + 2 * P


def route_block(nc, d, s, tab):
    with ExitStack() as ctx:
        def sb(name, shape, dt):
            return ctx.enter_context(nc.sbuf_tensor("route_" + name, shape, dt))

        def sem(name):
            return ctx.enter_context(nc.semaphore("route_" + name))

        ident = sb("ident", [P, P], F32)
        onesb = sb("onesb", [P, P], BF16)
        tri = sb("tri", [P, P], BF16)
        eps = sb("eps_col", [P, 1], F32)
        gw = sb("gw", [P, DC, E_N], F32)
        gwhi = sb("gwhi", [P, DC, E_N], F32R)
        gwlo = sb("gwlo", [P, DC, E_N], F32R)
        xn = sb("xn", [P, 2, TT, D], F32)
        stats = sb("stats", [P, TT, 6], F32)
        mv = sb("mv", [P, TT, 2], F32)
        rstd = sb("rstd", [P, TT], F32)
        nmr = sb("nmr", [P, TT], F32)
        pr = sb("pr", [P, TILES, E_N], F32)
        rest = sb("rest", [P, TILES, E_N], F32)
        mask = sb("mask", [P, TILES, E_N], BF16)
        before = sb("before", [P, TILES + 1, E_N], BF16)
        X = sb("X", [P, TILES, D], F32)
        xThi = sb("xThi", [P, DC, S], F32R)
        xTlo = sb("xTlo", [P, DC, S], F32R)
        wts = sb("wts", [P, TILES, E_N], F32)
        row = sb("row", [P, TILES, E_N], F32)
        ranki = sb("ranki", [P, TILES, E_N], I32)
        high = sb("high", [P, TILES, E_N], I32)
        highf = sb("highf", [P, TILES, E_N], F32)
        first_row = sb("first_row", [P, E_N], F32)
        first_rowi = sb("first_rowi", [P, E_N], I32)
        near = sb("near", [P, TILES, TOP], F32)
        same = sb("same", [P, TILES, TOP, E_N], F32)
        where = sb("where", [P, TILES, TOP], U32)
        entry = sb("entry", [P, TILES, TOP, 2], I32)
        blank = sb("blank", [P, E_N * CAP // P, 2], I32)
        zeros = sb("zeros", [P, 2, D], F32)
        cnt = sb("cnt", [P, E_N], F32)
        cnti = sb("cnti", [P, E_N], I32)
        pairs = sb("pairs", [P, 2 + E_N + 2], F32)
        ends = sb("ends", [P, 3, E_N + 2], F32)
        one_row = sb("one_row", [P, E_N + 2], F32)
        mx = sb("mx", [P, TILES], F32)
        top = sb("top", [P, TILES, TOP], F32)
        T = ctx.enter_context(nc.psum_tensor("route_T", [P, DC, S], F32))
        L = ctx.enter_context(nc.psum_tensor("route_L", [P, TILES, E_N], F32))
        R = ctx.enter_context(nc.psum_tensor("route_R", [P, TILES, E_N], F32))

        C = ctx.enter_context(nc.psum_tensor("route_C", [P, E_N], F32))
        tables_made = sem("tables_made")
        entries_made = sem("entries_made")
        blank_made = sem("blank_made")
        blank_out = sem("blank_out")
        rows_out = sem("rows_out")
        xn_out = [sem(f"xn_out{b}") for b in range(NB)]
        where_ready = sem("where_ready")
        sent = sem("sent")
        tab_ready = sem("tab_ready")
        x_in = [sem(f"x_in{b}") for b in range(NB)]
        g_in = sem("g_in")
        pool_made = sem("pool_made")
        dve_link = sem("dve_link")
        gw_split = sem("gw_split")
        var_ready = sem("var_ready")
        std_ready = sem("std_ready")
        rstd_ready = sem("rstd_ready")
        xn_ready = sem("xn_ready")
        xT_ready = sem("xT_ready")
        hi_ready = sem("hi_ready")
        lo_ready = sem("lo_ready")
        logits_ready = sem("logits_ready")
        shifted = sem("shifted")
        exp_ready = sem("exp_ready")
        mask_ready = sem("mask_ready")
        before_ready = sem("before_ready")
        rank_ready = sem("rank_ready")

        block = ctx.enter_context(nc.Block())

        @block.sync
        def _(sp):
            for b in range(NB):
                sp.dma_start(X[:, b * TT:(b + 1) * TT, :], s["X3"][b * S:(b + 1) * S, :].rearrange("(t p) n -> p t n", p=P)).then_inc(x_in[b], 16)
            sp.dma_start(gw[:, :, :], d["gw"].rearrange("(c p) e -> p c e", p=P)).then_inc(g_in, 16)
            sp.wait_ge(blank_made, 1)
            sp.dma_start(s["LIST"][0:E_N * CAP, :].rearrange("(p r) v -> p r v", p=P), blank[:, :, :]).then_inc(blank_out, 16)
            sp.dma_start(s["LIST"][E_N * CAP:, :].rearrange("(p r) v -> p r v", p=P), blank[:, 0:SUBS, :]).then_inc(blank_out, 16)
            sp.wait_ge(tables_made, 5)
            for name in ("X3", "XN"):
                sp.dma_start(s[name][NB * S:ROWS, :].rearrange("(t p) n -> p t n", p=P), zeros[:, :, :]).then_inc(rows_out, 16)
            for b in range(NB):
                sp.wait_ge(xn_ready, TT * b + TT)
                sp.dma_start(s["XN"][b * S:(b + 1) * S, :].rearrange("(t p) n -> p t n", p=P),
                             xn[:, b % 2, :, :]).then_inc(xn_out[b], 16)
            sp.wait_ge(rows_out, 32)
            for b in range(NB):
                sp.wait_ge(xn_out[b], 16)

        @block.gpsimd
        def _(pool):
            nc.gpsimd.memset(ident[:, :], 0.0).then_inc(pool_made, 1)
            nc.gpsimd.memset(onesb[:, :], 1.0).then_inc(pool_made, 1)
            nc.gpsimd.memset(tri[:, :], 1.0).then_inc(pool_made, 1)
            nc.gpsimd.memset(eps[:, :], EPS).then_inc(pool_made, 1)
            pool.wait_ge(pool_made, 4)
            nc.gpsimd.affine_select(out=ident[:, :], in_=ident[:, :], compare_op=ALU.not_equal, fill=1.0, base=0,
                                    pattern=[[-1, P]], channel_multiplier=1).then_inc(pool_made, 1)
            nc.gpsimd.memset(zeros[:, :, :], 0.0).then_inc(tables_made, 1)
            nc.gpsimd.memset(one_row[:, :], 1.0).then_inc(tables_made, 1)
            nc.gpsimd.iota(first_rowi[:, :], pattern=[[CAP, E_N]], base=0, channel_multiplier=0).then_inc(tables_made, 1)
            nc.gpsimd.iota(blank[:, :, 0], pattern=[[2, E_N * CAP // P // SUBS], [0, SUBS // 2], [1, 2]], base=0,
                           channel_multiplier=2 * E_N * CAP // P // SUBS).then_inc(tables_made, 1)
            nc.gpsimd.iota(entry[:, :, :, 0], pattern=[[P, TILES], [0, TOP]], base=0,
                           channel_multiplier=1).then_inc(tables_made, 1)
            nc.gpsimd.affine_select(out=tri[:, :], in_=tri[:, :], compare_op=ALU.is_gt, fill=0.0, base=0,
                                    pattern=[[1, P]], channel_multiplier=-1).then_inc(pool_made, 1)
            pool.wait_ge(blank_out, 32)
            pool.wait_ge(where_ready, 1)
            pool.wait_ge(entries_made, 1)
            for i in range(TILES):
                for k in range(TOP):
                    pool.indirect_dma_start(out=s["LIST"], out_offset=bass.IndirectOffsetOnAxis(ap=where[:, i, k:k + 1], axis=0),
                                            in_=entry[:, i, k, :], in_offset=None, bounds_check=E_N * CAP - 1,
                                            oob_is_err=False).then_inc(sent, 16)
            pool.wait_ge(sent, 16 * TILES * TOP)

        @block.tensor
        def _(pe):
            pe.wait_ge(pool_made, 6)
            pe.wait_ge(gw_split, 2)
            for b in range(NB):
                pe.wait_ge(xn_ready, TT * b + TT)
                if b > 0:
                    pe.wait_ge(lo_ready, b)
                if b > 0:
                    pe.wait_ge(logits_ready, b)
                for c in range(DC):
                    for t in range(TT):
                        last = nc.tensor.transpose(T[:, c, t * P:(t + 1) * P], xn[:, b % 2, t, c * P:(c + 1) * P], ident[:, :])
                last.then_inc(xT_ready, 1)
                pe.wait_ge(hi_ready, b + 1)
                pe.wait_ge(lo_ready, b + 1)
                for t in range(TT):
                    cols = slice(t * P, (t + 1) * P)
                    steps = [(c, x, g) for c in range(DC) for x, g in ((xThi, gwhi), (xTlo, gwhi), (xThi, gwlo))]
                    for i, (c, x, g) in enumerate(steps):
                        last = nc.tensor.matmul(L[:, b * TT + t, :], x[:, c, cols], g[:, c, :],
                                                start=(i == 0), stop=(i == len(steps) - 1))
                last.then_inc(logits_ready, 1)
            pe.wait_ge(mask_ready, 1)
            pe.wait_ge(before_ready, TILES)
            for i in range(TILES):
                last = nc.tensor.matmul(R[:, i, :], tri[:, :], mask[:, i, :], start=True, stop=(i == 0))
                if i > 0:
                    last = nc.tensor.matmul(R[:, i, :], onesb[:, :], before[:, i, :], start=False, stop=True)
            nc.tensor.matmul(C[:, :], onesb[:, :], before[:, TILES, :], start=True, stop=True).then_inc(rank_ready, 1)

        @block.scalar
        def _(act):
            act.wait_ge(pool_made, 6)
            for b in range(NB):
                act.wait_ge(var_ready, TT * b + TT)
                nc.scalar.activation(rstd[:, :], mv[:, :, 1], ACT.Sqrt, bias=eps[:, :]).then_inc(std_ready, 1)
                act.wait_ge(rstd_ready, b + 1)
                if b >= 2:
                    act.wait_ge(xT_ready, b - 1)
                    act.wait_ge(xn_out[b - 2], 16)
                for t in range(TT):
                    nc.scalar.activation(xn[:, b % 2, t, :], X[:, b * TT + t, :], ACT.Identity, bias=nmr[:, t:t + 1],
                                         scale=rstd[:, t:t + 1]).then_inc(xn_ready, 1)
                act.wait_ge(xT_ready, b + 1)
                nc.scalar.activation(xThi[:, :, :], T[:, :, :], ACT.Copy).then_inc(hi_ready, 1)
            act.wait_ge(shifted, 1)
            nc.scalar.activation(pr[:, :, :], pr[:, :, :], ACT.Exp).then_inc(exp_ready, 1)

        @block.vector
        def _(dve):
            link = Link(dve, dve_link)
            dve.wait_ge(tables_made, 5)
            link(nc.vector.memset(blank[:, :, 1], 0))
            link(nc.vector.tensor_scalar(blank[:, :, 0], blank[:, :, 0], 2 * P - 1, None, ALU.bitwise_and))
            nc.vector.tensor_scalar(blank[:, :, 0], blank[:, :, 0], float(NB * S), None, ALU.add).then_inc(blank_made, 1)
            dve.wait_ge(g_in, 16)
            nc.vector.tensor_copy(gwhi[:, :, :], gw[:, :, :]).then_inc(gw_split, 1)
            dve.wait_ge(gw_split, 1)
            nc.vector.tensor_tensor(gwlo[:, :, :], gw[:, :, :], gwhi[:, :, :].bitcast(F32), ALU.subtract).then_inc(gw_split, 1)
            for b in range(NB):
                dve.wait_ge(x_in[b], 16)
                for t in range(TT):
                    link(nc.vector.bn_stats(stats[:, t, :], X[:, b * TT + t, :]))
                if b > 0:
                    dve.wait_ge(xn_ready, TT * b)
                for t in range(TT):
                    nc.vector.bn_aggr(mv[:, t, :], stats[:, t, :]).then_inc(var_ready, 1)
                dve.wait_ge(std_ready, b + 1)
                link(nc.vector.reciprocal(rstd[:, :], rstd[:, :]))
                nc.vector.scalar_tensor_tensor(out=nmr[:, :], in0=mv[:, :, 0], scalar=-1.0, in1=rstd[:, :],
                                               op0=ALU.mult, op1=ALU.mult).then_inc(rstd_ready, 1)
                dve.wait_ge(hi_ready, b + 1)
                nc.vector.tensor_tensor(xTlo[:, :, :], T[:, :, :],
                                        xThi[:, :, :].bitcast(F32), ALU.subtract).then_inc(lo_ready, 1)
            dve.wait_ge(logits_ready, NB)
            def over(m):
                return m.unsqueeze(2).to_broadcast([P, TILES, E_N])
            link(nc.vector.tensor_reduce(mx[:, :], L[:, :, :], AX_X, ALU.max))
            nc.vector.tensor_tensor(pr[:, :, :], L[:, :, :], over(mx[:, :]), ALU.subtract).then_inc(shifted, 1)
            dve.wait_ge(exp_ready, 1)
            link(nc.vector.tensor_reduce(mx[:, :], pr[:, :, :], AX_X, ALU.add))
            link(nc.vector.reciprocal(mx[:, :], mx[:, :]))
            link(nc.vector.tensor_tensor(pr[:, :, :], pr[:, :, :], over(mx[:, :]), ALU.mult))
            for i in range(TILES):
                link(nc.vector.max(top[:, i, :], pr[:, i, :]))
            for i in range(TILES):
                link(nc.vector.match_replace(rest[:, i, :], top[:, i, :], pr[:, i, :], -1.0))
            nc.vector.tensor_scalar(mask[:, :, :], rest[:, :, :], 0.0, None, ALU.is_lt).then_inc(mask_ready, 1)
            dve.wait_ge(mask_ready, 1)
            for i in range(1, TILES + 1):
                if i == 1:
                    nc.vector.tensor_copy(before[:, 1, :], mask[:, 0, :]).then_inc(before_ready, 1)
                else:
                    nc.vector.tensor_tensor(before[:, i, :], before[:, i - 1, :], mask[:, i - 1, :],
                                            ALU.add).then_inc(before_ready, 1)
                dve.wait_ge(before_ready, i)
            link(nc.vector.tensor_reduce(mx[:, :], top[:, :, :], AX_X, ALU.add))
            link(nc.vector.reciprocal(mx[:, :], mx[:, :]))
            link(nc.vector.tensor_tensor(pr[:, :, :], pr[:, :, :], over(mx[:, :]), ALU.mult))
            link(nc.vector.tensor_tensor(pr[:, :, :], pr[:, :, :], mask[:, :, :], ALU.mult))
            dve.wait_ge(rank_ready, 1)
            link(nc.vector.scalar_tensor_tensor(out=wts[:, :, :], in0=R[:, :, :], scalar=float(CAP), in1=pr[:, :, :],
                                                op0=ALU.is_lt, op1=ALU.mult))
            link(nc.vector.scalar_tensor_tensor(out=rest[:, :, :], in0=R[:, :, :], scalar=float(CAP), in1=mask[:, :, :],
                                                op0=ALU.is_lt, op1=ALU.mult))
            link(nc.vector.tensor_copy(ranki[:, :, :], R[:, :, :]))
            link(nc.vector.tensor_scalar(high[:, :, :], ranki[:, :, :], 7, None, ALU.arith_shift_right))
            link(nc.vector.tensor_scalar(highf[:, :, :], high[:, :, :], -float(P * SUBS - 1), None, ALU.mult))
            link(nc.vector.scalar_tensor_tensor(out=row[:, :, :], in0=R[:, :, :], scalar=float(SUBS), in1=highf[:, :, :],
                                                op0=ALU.mult, op1=ALU.add))
            dve.wait_ge(tables_made, 5)
            link(nc.vector.tensor_copy(first_row[:, :], first_rowi[:, :]))
            link(nc.vector.tensor_tensor(row[:, :, :], row[:, :, :],
                                         first_row[:, :].unsqueeze(1).to_broadcast([P, TILES, E_N]), ALU.add))
            link(nc.vector.tensor_scalar(row[:, :, :], row[:, :, :], -1.0, AWAY, ALU.mult, ALU.add))
            link(nc.vector.tensor_tensor(row[:, :, :], row[:, :, :], rest[:, :, :], ALU.mult))
            for i in range(TILES):
                link(nc.vector.max(near[:, i, :], row[:, i, :]))
            nc.vector.tensor_scalar(where[:, :, :], near[:, :, :], -1.0, AWAY, ALU.mult, ALU.add).then_inc(where_ready, 1)
            link(nc.vector.tensor_tensor(same[:, :, :, :], row[:, :, :].unsqueeze(2).to_broadcast([P, TILES, TOP, E_N]),
                                         near[:, :, :].unsqueeze(3).to_broadcast([P, TILES, TOP, E_N]), ALU.is_equal))
            link(nc.vector.tensor_tensor(same[:, :, :, :], same[:, :, :, :],
                                         wts[:, :, :].unsqueeze(2).to_broadcast([P, TILES, TOP, E_N]), ALU.mult))
            nc.vector.tensor_reduce(entry[:, :, :, 1].bitcast(F32), same[:, :, :, :], AX_X, ALU.add).then_inc(entries_made, 1)
            link(nc.vector.tensor_scalar(cnt[:, :], C[:, :], float(CAP), 2.0 * P - 1.0, ALU.min, ALU.add))
            link(nc.vector.tensor_copy(cnti[:, :], cnt[:, :]))
            link(nc.vector.tensor_scalar(cnti[:, :], cnti[:, :], 8, None, ALU.arith_shift_right))
            link(nc.vector.memset(pairs[:, :], 0.0))
            link(nc.vector.tensor_scalar(pairs[:, 0:E_N], cnti[:, :], 1.0, None, ALU.max))
            link(nc.vector.memset(ends[:, :, :], 0.0))
            link(nc.vector.tensor_tensor_scan(ends[:, 1, :], one_row[:, :], pairs[:, 0:E_N + 2], 0.0, ALU.mult, ALU.add))
            for q in range(2):
                link(nc.vector.tensor_tensor_scan(ends[:, 2, q::2], one_row[:, q::2], pairs[:, q:E_N + 2:2], 0.0,
                                                  ALU.mult, ALU.add))
            link(nc.vector.tensor_tensor(ends[:, 1, :], ends[:, 1, :], pairs[:, 0:E_N + 2], ALU.subtract))
            link(nc.vector.tensor_copy(ends[:, 0, :], pairs[:, 0:E_N + 2]))
            nc.vector.tensor_copy(tab[:, :, :], ends[0:1, :, :]).then_inc(tab_ready, 1)


def expert_block(nc, d, s, out, tab):
    with ExitStack() as ctx:
        sems = []

        def sb(name, shape, dt):
            return ctx.enter_context(nc.sbuf_tensor("moe_" + name, shape, dt))

        def ps(name, shape, dt):
            return ctx.enter_context(nc.psum_tensor("moe_" + name, shape, dt))

        def dma_sem(name):
            return ctx.enter_context(nc.semaphore("moe_" + name))

        def sem(name):
            sems.append(dma_sem(name))
            return sems[-1]

        ident = sb("ident", [P, P], F32)
        raw = sb("raw", [P, EW + 2 * D], F32)
        whi = sb("whi", [P, 2, EW + 2 * D], F32R)
        wlo = sb("wlo", [P, 2, EW + 2 * D], F32R)
        ids_g = sb("ids_g", [P, 2, SUBS, 2], I32)
        ids_s = sb("ids_s", [P, 2, SUBS, 2], I32)
        xg = sb("xg", [P, 2, SUBS, D], F32)
        xhi = sb("xhi", [P, 2, D], F32R)
        xlo = sb("xlo", [P, 2, D], F32R)
        th = sb("th", [P, 2, F], F32)
        h = sb("h", [P, 2, 2 * P], F32)
        hhi = sb("hhi", [P, 2, 2 * P], F32R)
        hlo = sb("hlo", [P, 2, 2 * P], F32R)
        wcol = sb("wcol", [P, 2], F32)
        ys = sb("ys", [P, 2, D], F32)
        fence = sb("fence", [P, 2], F32)
        T = ps("T", [P, 2, D], F32)
        G = ps("G", [P, 2, 512], F32)
        H = ps("H", [P, 2, 512], F32)
        Y = ps("Y", [P, 2, D], F32)

        pool_made = sem("pool_made")
        raw_in = sem("raw_in")
        ids_g_in = sem("ids_g_in")
        ids_s_in = sem("ids_s_in")
        whi_ready = sem("whi_ready")
        wlo_ready = sem("wlo_ready")
        gathered = [dma_sem(f"gathered{q}") for q in range(2)]
        added = [dma_sem(f"added{q}") for q in range(2)]
        stood = sem("stood")
        xT_ready = sem("xT_ready")
        xhi_ready = sem("xhi_ready")
        xlo_ready = sem("xlo_ready")
        gu_ready = sem("gu_ready")
        tanh_ready = sem("tanh_ready")
        gated = sem("gated")
        h_ready = sem("h_ready")
        hT_ready = sem("hT_ready")
        hhi_ready = sem("hhi_ready")
        hlo_ready = sem("hlo_ready")
        y_ready = sem("y_ready")
        wcol_ready = sem("wcol_ready")
        ys_ready = sem("ys_ready")
        x_out = sem("x_out")
        start_up(nc, sems)
        block = ctx.enter_context(nc.Block())

        MOST = NB * S * TOP // (2 * P) + E_N

        def at_least(e):
            return max(e, 0) if isinstance(e, int) else 1

        def pairs_of(eng, e):
            return eng.value_load(tab[0:1, 0, bass.ds(e, 1)], min_val=0, max_val=PAIRS)

        def base_of(eng, e):
            return eng.value_load(tab[0:1, 1, bass.ds(e, 1)], min_val=at_least(e), max_val=MOST)

        def parity_end_of(eng, e):
            return eng.value_load(tab[0:1, 2, bass.ds(e, 1)], min_val=1, max_val=MOST)

        def all_experts(eng, expert):
            expert(0, 0)
            expert(1, 1)
            with eng.Fori(1, E_N // 2) as j:
                for q in range(2):
                    expert(j * 2 + q, q)

        def all_pairs(eng, n, base, pair, between=None):
            pair(0, base)
            if between:
                between(base)
            for i in range(1, PAIRS):
                with eng.If(n > i):
                    pair(i, base + i)

        def is_first(e, i):
            return isinstance(e, int) and e == 0 and i == 0

        @block.sync
        def _(sp):
            def load_raw(e):
                sp.dma_start(raw[:, :], d["ew"][e]).then_inc(raw_in, 16)

            def load_ids(dst, at, e, ready):
                sp.dma_start(dst[:, at, :, :], s["LIST"].rearrange("(e p r) v -> e p r v", e=E_N + 1, p=P)[e]).then_inc(ready, 16)

            load_raw(0)
            load_ids(ids_g, 0, 0, ids_g_in)

            def expert(e, q):
                if not (isinstance(e, int) and e == 0):
                    end, base_before = parity_end_of(sp, e - 1), base_of(sp, e - 1)
                    sp.wait_ge(gathered[1 - q], end * 32)
                need(sp, ids_g_in, 16 * (e + 1))
                load_ids(ids_g, 1 - q, e + 1, ids_g_in)
                if not isinstance(e, int):
                    for k in range(2):
                        sp.wait_ge(added[k], base_before * 16 + 16)
                need(sp, ids_s_in, 16 * e)
                load_ids(ids_s, q, e, ids_s_in)
                need(sp, whi_ready, e + 1)
                need(sp, wlo_ready, e + 1)
                load_raw(e + 1)

            all_experts(sp, expert)
            total = base_of(sp, E_N)
            for k in range(2):
                sp.wait_ge(added[k], total * 16 + 16)
            sp.dma_start(out.rearrange("b s n -> (b s) n"), s["X3"][0:NB * S, :]).then_inc(x_out, 16)
            need(sp, x_out, 16)

        @block.gpsimd
        def _(pool):
            nc.gpsimd.memset(ident[:, :], 0.0).then_inc(pool_made, 1)
            nc.gpsimd.memset(fence[:, :], 0.0).then_inc(pool_made, 1)
            nc.gpsimd.memset(h[:, :, F:2 * P], 0.0).then_inc(pool_made, 1)
            need(pool, pool_made, 3)
            nc.gpsimd.affine_select(out=ident[:, :], in_=ident[:, :], compare_op=ALU.not_equal, fill=1.0, base=0,
                                    pattern=[[-1, P]], channel_multiplier=1).then_inc(pool_made, 1)
            for k in range(2):
                pool.dma_start(ys[:, k, :], s["XN"][k * P:(k + 1) * P, :]).then_inc(added[k], 16)

            def stand(n, more):
                need(pool, stood, n, more)
                nc.gpsimd.tensor_tensor(fence[:, 0:1], fence[:, 1:2], fence[:, 1:2], ALU.add).then_inc(stood, 1)

            def gather(e, q, n, base):
                need(pool, ids_g_in, 16 * (e + 1))
                stand(base * 2 + e, 0)
                for i in range(PAIRS):
                    with pool.If(n > i):
                        for r in (2 * i, 2 * i + 1):
                            pool.indirect_dma_start(
                                out=xg[:, q, r, :], out_offset=None, in_=s["XN"],
                                in_offset=bass.IndirectOffsetOnAxis(ap=ids_g[:, q, r, 0:1].bitcast(U32), axis=0),
                                bounds_check=ROWS - 1).then_inc(gathered[q], 16)

            gather(0, 0, pairs_of(pool, 0), 0)

            def expert(e, q):
                n, n_next, base = pairs_of(pool, e), pairs_of(pool, e + 1), base_of(pool, e)
                if not (isinstance(e, int) and e == 0):
                    need(pool, xT_ready, base * 2)
                gather(e + 1, 1 - q, n_next, base)
                need(pool, ids_s_in, 16 * (e + 1))

                def pair(i, g):
                    if i == 0:
                        for k in range(2):
                            pool.wait_ge(added[k], g * 16 + 16)
                    for k in range(2):
                        need(pool, ys_ready, g * 2, k + 1)
                        stand(g * 2 + e, k + 2)
                        pool.indirect_dma_start(
                            out=s["X3"], in_=ys[:, k, :], in_offset=None,
                            out_offset=bass.IndirectOffsetOnAxis(ap=ids_s[:, q, 2 * i + k, 0:1].bitcast(U32), axis=0),
                            bounds_check=ROWS - 1, compute_op=ALU.add).then_inc(added[k], 16)

                all_pairs(pool, n, base, pair)

            all_experts(pool, expert)

        @block.tensor
        def _(pe):
            need(pe, pool_made, 4)

            def down(k, g, wq, back=0):
                need(pe, hhi_ready, g * 2, k + 1 - 2 * back)
                need(pe, hlo_ready, g * 2, k + 1 - 2 * back)
                need(pe, ys_ready, g * 2, k - 1 - 2 * back)
                steps = [(r, a, w) for r in range(2) for a, w in ((hhi, whi), (hlo, whi), (hhi, wlo))]
                for i, (r, a, w) in enumerate(steps):
                    last = nc.tensor.matmul(Y[:, k, :], a[:, k, r * P:(r + 1) * P], w[:, wq, EW + r * D:EW + (r + 1) * D],
                                            start=(i == 0), stop=(i == len(steps) - 1))
                last.then_inc(y_ready, 1)

            def hidden_transposes(k, g, back=0):
                need(pe, h_ready, g * 2, k + 1 - 2 * back)
                for r in range(2):
                    last = nc.tensor.transpose(H[:, k, r * P:(r + 1) * P], h[:, k, r * P:(r + 1) * P], ident[:, :])
                last.then_inc(hT_ready, 1)

            def expert(e, q):
                n, base, end = pairs_of(pe, e), base_of(pe, e), parity_end_of(pe, e)
                need(pe, whi_ready, e + 1)
                need(pe, wlo_ready, e + 1)
                pe.wait_ge(gathered[q], end * 32)

                def pair(i, g):
                    wq = 1 - q if i == 0 else q
                    for k in range(2):
                        need(pe, xlo_ready, g * 2, k - 1)
                        for c in range(DC):
                            last = nc.tensor.transpose(T[:, k, c * P:(c + 1) * P], xg[:, q, 2 * i + k, c * P:(c + 1) * P],
                                                       ident[:, :])
                        last.then_inc(xT_ready, 1)
                        if not is_first(e, i):
                            down(k, g, wq, 1)
                        if k == 1:
                            hidden_transposes(0, g)
                        elif not is_first(e, i):
                            hidden_transposes(1, g, 1)
                        need(pe, xlo_ready, g * 2, k + 1)
                        need(pe, h_ready, g * 2, k - 1)
                        steps = [(c, a, w) for c in range(DC) for a, w in ((xhi, whi), (xlo, whi), (xhi, wlo))]
                        for m, (c, a, w) in enumerate(steps):
                            last = nc.tensor.matmul(G[:, k, 0:GUC], a[:, k, c * P:(c + 1) * P],
                                                    w[:, q, c * GUC:(c + 1) * GUC],
                                                    start=(m == 0), stop=(m == len(steps) - 1))
                        last.then_inc(gu_ready, 1)

                all_pairs(pe, n, base, pair)

            all_experts(pe, expert)
            total = base_of(pe, E_N)
            down(0, total, 1, 1)
            hidden_transposes(1, total, 1)
            down(1, total, 1, 1)

        @block.scalar
        def _(act):
            def split(e, q):
                need(act, raw_in, 16 * (e + 1))
                nc.scalar.activation(whi[:, q, :], raw[:, :], ACT.Copy).then_inc(whi_ready, 1)

            split(0, 0)

            def result(k, g, back=0):
                need(act, y_ready, g * 2, k + 1 - 2 * back)
                act.wait_ge(added[k], g * 16 + (16 - 16 * back))
                need(act, wcol_ready, g * 2, k + 1 - 2 * back)
                nc.scalar.activation(ys[:, k, :], Y[:, k, :], ACT.Copy, scale=wcol[:, k:k + 1]).then_inc(ys_ready, 1)

            def hidden_high(k, g, back=0):
                need(act, hT_ready, g * 2, k + 1 - 2 * back)
                nc.scalar.activation(hhi[:, k, :], H[:, k, 0:2 * P], ACT.Copy).then_inc(hhi_ready, 1)

            def expert(e, q):
                n, base = pairs_of(act, e), base_of(act, e)
                need(act, ids_s_in, 16 * (e + 1))

                def pair(i, g):
                    for k in range(2):
                        need(act, xT_ready, g * 2, k + 1)
                        need(act, gu_ready, g * 2, k - 1)
                        nc.scalar.activation(xhi[:, k, :], T[:, k, :], ACT.Copy).then_inc(xhi_ready, 1)
                        if not is_first(e, i):
                            result(k, g, 1)
                        if k == 1:
                            hidden_high(0, g)
                        elif not is_first(e, i):
                            hidden_high(1, g, 1)
                        need(act, gu_ready, g * 2, k + 1)
                        nc.scalar.activation(th[:, k, 0:P], G[:, k, 0:P], ACT.Tanh, scale=0.5)
                        nc.scalar.activation(th[:, k, P:F], G[:, k, 2 * P:2 * P + F2], ACT.Tanh, scale=0.5).then_inc(tanh_ready, 1)
                        need(act, ys_ready, g * 2, k - 1)
                        nc.scalar.activation(wcol[:, k:k + 1], ids_s[:, q, 2 * i + k, 1:2].bitcast(F32),
                                             ACT.Copy).then_inc(wcol_ready, 1)

                def between(base):
                    if not (isinstance(e, int) and e == 0):
                        need(act, y_ready, base * 2)
                    split(e + 1, 1 - q)

                all_pairs(act, n, base, pair, between)

            all_experts(act, expert)
            total = base_of(act, E_N)
            result(0, total, 1)
            hidden_high(1, total, 1)
            result(1, total, 1)

        @block.vector
        def _(dve):
            def split(e, q):
                need(dve, whi_ready, e + 1)
                nc.vector.tensor_tensor(wlo[:, q, :], raw[:, :], whi[:, q, :].bitcast(F32), ALU.subtract).then_inc(wlo_ready, 1)

            split(0, 0)
            need(dve, pool_made, 4)

            def hidden_low(k, g, back=0):
                need(dve, hhi_ready, g * 2, k + 1 - 2 * back)
                nc.vector.tensor_tensor(hlo[:, k, :], H[:, k, 0:2 * P], hhi[:, k, :].bitcast(F32),
                                        ALU.subtract).then_inc(hlo_ready, 1)

            def expert(e, q):
                n, base = pairs_of(dve, e), base_of(dve, e)

                def pair(i, g):
                    for k in range(2):
                        need(dve, xhi_ready, g * 2, k + 1)
                        nc.vector.tensor_tensor(xlo[:, k, :], T[:, k, :], xhi[:, k, :].bitcast(F32),
                                                ALU.subtract).then_inc(xlo_ready, 1)
                        if k == 1:
                            hidden_low(0, g)
                        elif not is_first(e, i):
                            hidden_low(1, g, 1)
                        need(dve, tanh_ready, g * 2, k + 1)
                        need(dve, hT_ready, g * 2, k - 1)
                        for a, o in ((0, 0), (2 * P, P)):
                            n = P if a == 0 else F2
                            last = nc.vector.scalar_tensor_tensor(out=th[:, k, o:o + n], in0=th[:, k, o:o + n], scalar=1.0,
                                                                  in1=G[:, k, a:a + n], op0=ALU.add, op1=ALU.mult)
                        last.then_inc(gated, 1)
                        need(dve, gated, g * 2, k + 1)
                        for a, o in ((P, 0), (2 * P + F2, P)):
                            n = P if a == P else F2
                            last = nc.vector.scalar_tensor_tensor(out=h[:, k, o:o + n], in0=th[:, k, o:o + n], scalar=0.5,
                                                                  in1=G[:, k, a:a + n], op0=ALU.mult, op1=ALU.mult)
                        last.then_inc(h_ready, 1)

                def between(base):
                    split(e + 1, 1 - q)

                all_pairs(dve, n, base, pair, between)

            all_experts(dve, expert)
            hidden_low(1, base_of(dve, E_N), 1)




def build(nc, d, out, stage=None):
    s = {
        "W": nc.dram_tensor("w_halves", [CH, P, 2 * WCH], F32).ap(),
        "BC": nc.dram_tensor("bc_rows", [NB, 2 * NST, S], F32).ap(),
        "U": nc.dram_tensor("u_store", [NB, P, DC, S], F32).ap(),
        "DT": nc.dram_tensor("dt_store", [NB, P, DC, S], F32).ap(),
        "DU": nc.dram_tensor("du_store", [NB, P, DC, S], F32).ap(),
        "X1": nc.dram_tensor("x1_store", [NB, S, D], F32).ap(),
        "X3": nc.dram_tensor("x3_store", [ROWS, D], F32).ap(),
        "XN": nc.dram_tensor("xn_store", [ROWS, D], F32).ap(),
        "LIST": nc.dram_tensor("lists", [(E_N + 1) * CAP, 2], I32).ap(),
    }
    prepare_block(nc, d, s)
    quant_block(nc, d, s)
    mix_block(nc, d, s)
    with ExitStack() as ctx:
        tab = ctx.enter_context(nc.sbuf_tensor("tab", [1, 3, E_N + 2], I32))
        route_block(nc, d, s, tab)
        expert_block(nc, d, s, out, tab)


def lay_out(inputs):
    import numpy as np

    g = {k: np.asarray(v) for k, v in inputs.items()}
    idx = np.zeros((CH, P, WCH), np.int32)
    for j in range(CH):
        n = min(P, INTER - j * P)
        rows = slice(j * P, j * P + n)
        for q, name in enumerate(("L0_ffn_gate_idx", "L0_ffn_up_idx")):
            part = g[name][rows].T.reshape(DC, P, n).transpose(1, 0, 2)
            idx[j, :, q * D:(q + 1) * D].reshape(P, DC, P)[:, :, :n] = part
        idx[j, :n, 2 * D:] = g["L0_ffn_down_idx"][:, rows].T
    ew = np.zeros((E_N + 1, P, EW + 2 * D), np.float32)
    gu = ew[:E_N, :, :EW].reshape(E_N, P, DC, GUC)
    gate, up = (g[k].reshape(E_N, DC, P, F).transpose(0, 2, 1, 3) for k in ("L1_ffn_w_gate", "L1_ffn_w_up"))
    gu[..., :P], gu[..., P:2 * P] = gate[..., :P], up[..., :P]
    gu[..., 2 * P:2 * P + F2], gu[..., 2 * P + F2:] = gate[..., P:], up[..., P:]
    ew[:E_N, :, EW:EW + D] = g["L1_ffn_w_down"][:, :P]
    ew[:E_N, :F2, EW + D:] = g["L1_ffn_w_down"][:, P:]
    c = np.ascontiguousarray
    return {
        "x": g["x"], "fw": g["fside_BxS2xS2_0"], "ctx": g["ctx_1024"],
        "ctxT": c(g["ctx_1024"].transpose(0, 2, 1)), "lut": g["L0_ffn_lut"], "idx": idx,
        "inT": c(g["L1_xattn_in_proj_w"].T), "xpT": c(g["L1_xattn_x_proj_w"].T), "dpT": c(g["L1_xattn_dt_proj_w"].T),
        "convw": c(g["L1_xattn_conv_w"][:, 0, :]), "convb": c(g["L1_xattn_conv_b"].reshape(DC, P).T),
        "dtb": c(g["L1_xattn_dt_proj_b"].reshape(DC, P).T),
        "alog": c(g["L1_xattn_A_log"].reshape(DC, P, NST).transpose(1, 0, 2)),
        "dskip": c(g["L1_xattn_D"].reshape(DC, P).T),
        "gw": g["L1_ffn_gate_w"], "ew": ew,
    }


def kernel(**inputs):
    import numpy as np
    import concourse.bacc as bacc
    from concourse.bass_utils import run_bass_kernel_spmd as run

    nc = bacc.Bacc("TRN2", target_bir_lowering=False, num_devices=1)
    arrays, d = {}, {}
    for name, a in lay_out(inputs).items():
        arrays[f"in_{name}"] = a
        d[name] = nc.dram_tensor(f"in_{name}", a.shape, mybir.dt.from_np(a.dtype), kind="ExternalInput").ap()
    out = nc.dram_tensor("out_x", [NB, S, D], F32, kind="ExternalOutput").ap()
    build(nc, d, out)
    r = run(nc, [arrays], core_ids=[0])
    return r.results[0]["out_x"]
```
